# Optimizing a Trainium2 kernel written in Bass

```python
import numpy as np
import jax
import jax.numpy as jnp

def _softmax(x, axis=-1):
    return jax.nn.softmax(x, axis=axis)

def _gelu(x):
    return jax.nn.gelu(x, approximate=True)

def _silu(x):
    return jax.nn.silu(x)

def _sigmoid(x):
    return jax.nn.sigmoid(x)

def _layernorm(x, axis=-1, eps=1e-05):
    m = jnp.mean(x, axis=axis, keepdims=True)
    v = jnp.var(x, axis=axis, keepdims=True)
    return (x - m) / jnp.sqrt(v + eps)

def _scatter_add(tgt, idx, src, axis=0):
    return tgt.at[idx].add(src)

def _segment_sum(src, seg, n):
    return jax.ops.segment_sum(src, seg, n)
kernel_name = 'mk_gnn_preln_d1_gnn_r64_24cd24'

def setup_inputs(seed: int=0):
    np.random.seed(seed)
    _w = jnp.asarray

    def _rec_inputs():
        import jax
        import jax.numpy as jnp
        _gk = jax.random.key(seed)
        x = -0.000202 + 1 * jax.random.normal(jax.random.fold_in(_gk, 1), (100000, 128), jnp.float32)
        src = jax.random.randint(jax.random.fold_in(_gk, 2), (25000,), 0, 100000, jnp.int32)
        dst = jax.random.randint(jax.random.fold_in(_gk, 3), (25000,), 0, 100000, jnp.int32)
        _o = jnp.argsort(dst, stable=True)
        src = src[_o]
        dst = dst[_o]
        edge_attr_50 = 0.000154925 + 1.00009 * jax.random.normal(jax.random.fold_in(_gk, 11), (25000, 50), jnp.float32)
        edge_weight = jax.random.uniform(jax.random.fold_in(_gk, 13), (25000,), jnp.float32, 0.0, 0.999998)
        return (x, src, dst, edge_attr_50, edge_weight)
    x, src, dst, edge_attr_50, edge_weight = _rec_inputs()

    def _L0_gnn_setup():
        import jax, jax.numpy as jnp
        import numpy as np
        N_NODES = 50000
        N_EDGES = 12500
        HIDDEN = 128
        NUM_FILTERS = 128
        NUM_GAUSSIANS = 50
        key = jax.random.key(seed)
        ks = jax.random.split(key, 8)
        h = jax.random.normal(ks[0], (N_NODES, HIDDEN), dtype=jnp.float32)
        edge_index = jax.random.randint(ks[1], (2, N_EDGES), 0, N_NODES, dtype=jnp.int64)
        edge_weight = jax.random.uniform(ks[2], (N_EDGES,), dtype=jnp.float32)
        edge_attr = jax.random.normal(ks[3], (N_EDGES, NUM_GAUSSIANS), dtype=jnp.float32)
        s1 = 1.0 / np.sqrt(NUM_GAUSSIANS)
        s2 = 1.0 / np.sqrt(NUM_FILTERS)
        s3 = 1.0 / np.sqrt(HIDDEN)
        mlp_w1 = jax.random.normal(ks[4], (NUM_GAUSSIANS, NUM_FILTERS), dtype=jnp.float32) * s1
        mlp_b1 = jnp.zeros((NUM_FILTERS,), dtype=jnp.float32)
        mlp_w2 = jax.random.normal(ks[5], (NUM_FILTERS, HIDDEN), dtype=jnp.float32) * s2
        mlp_b2 = jnp.zeros((HIDDEN,), dtype=jnp.float32)
        lin_w = jax.random.normal(ks[6], (HIDDEN, HIDDEN), dtype=jnp.float32) * s3
        lin_b = jnp.zeros((HIDDEN,), dtype=jnp.float32)
        return {'h': h, 'edge_index': edge_index, 'edge_weight': edge_weight, 'edge_attr': edge_attr, 'mlp_w1': mlp_w1, 'mlp_b1': mlp_b1, 'mlp_w2': mlp_w2, 'mlp_b2': mlp_b2, 'lin_w': lin_w, 'lin_b': lin_b}
    _L0_gnn_all = _L0_gnn_setup()
    _L0_gnn_in = {k: v for k, v in _L0_gnn_all.items() if k in ('mlp_w1', 'mlp_b1', 'mlp_w2', 'mlp_b2', 'lin_w', 'lin_b')}
    del _L0_gnn_all
    return {'x': x, 'src': src, 'dst': dst, 'edge_attr_50': edge_attr_50, 'edge_weight': edge_weight, 'L0_gnn_mlp_w1': _L0_gnn_in['mlp_w1'], 'L0_gnn_mlp_b1': _L0_gnn_in['mlp_b1'], 'L0_gnn_mlp_w2': _L0_gnn_in['mlp_w2'], 'L0_gnn_mlp_b2': _L0_gnn_in['mlp_b2'], 'L0_gnn_lin_w': _L0_gnn_in['lin_w'], 'L0_gnn_lin_b': _L0_gnn_in['lin_b']}

def reference(x, src, dst, edge_attr_50, edge_weight, L0_gnn_mlp_w1, L0_gnn_mlp_b1, L0_gnn_mlp_w2, L0_gnn_mlp_b2, L0_gnn_lin_w, L0_gnn_lin_b):
    import jax
    import jax.numpy as jnp

    def _L0_gnn_ref(h, edge_index, edge_weight, edge_attr, mlp_w1, mlp_b1, mlp_w2, mlp_b2, lin_w, lin_b):
        import jax, jax.numpy as jnp
        import numpy as np
        N_NODES = 50000
        N_EDGES = 12500
        HIDDEN = 128
        NUM_FILTERS = 128
        NUM_GAUSSIANS = 50
        W = jax.nn.relu(edge_attr @ mlp_w1 + mlp_b1) @ mlp_w2 + mlp_b2
        src = edge_index[0]
        dst = edge_index[1]
        messages = W * h[dst]
        agg = jax.ops.segment_sum(messages, src, num_segments=h.shape[0])
        h_new = h + agg
        return h_new @ lin_w + lin_b
    edge_index = jnp.stack([src, dst])
    h = jnp.maximum(_layernorm(x, axis=-1), 0.0)
    x = x + _L0_gnn_ref(h, edge_index, edge_weight, edge_attr_50, L0_gnn_mlp_w1, L0_gnn_mlp_b1, L0_gnn_mlp_w2, L0_gnn_mlp_b2, L0_gnn_lin_w, L0_gnn_lin_b)
    return x

_drawn_inputs = setup_inputs


def setup_inputs(seed=0):
    import zlib

    import numpy as np

    out = dict(_drawn_inputs(seed))
    spreads = {'L0_gnn_mlp_b1': (0.0, 0.399), 'L0_gnn_mlp_b2': (0.0, 0.297), 'L0_gnn_lin_b': (0.0, 0.1)}
    factors = {}
    for name, (base, spread) in spreads.items():
        noise = np.random.default_rng([zlib.crc32(name.encode()), seed]).standard_normal(out[name].shape)
        drawn = base * np.exp(spread * noise) if base else spread * noise
        out[name] = jnp.asarray(drawn.astype(out[name].dtype))
    for name, factor in factors.items():
        out[name] = (out[name] * factor).astype(out[name].dtype)
    return out
```

```python
from contextlib import ExitStack

import concourse.bass as bass
from concourse import mybir

P = 128
F32 = mybir.dt.float32
BF16 = mybir.dt.bfloat16
I32 = mybir.dt.int32
ALU = mybir.AluOpType
ACT = mybir.ActivationFunctionType
AX_X = mybir.AxisListType.X

D = 128
QUAD = 4
BATCH = 16
QUADS = BATCH // QUAD
XSLOTS = 4
EPS = 1e-5
IN_FLIGHT = 3
TOP = 8
ACT_NORM = 2


def node_tiles(nodes):
    return -(-nodes // (P * BATCH)) * BATCH


def edge_tiles(edges):
    return -(-edges // (P * QUAD)) * QUAD


def build(nc, x, src_cols, src_rows, dst_cols, attr_t, w1, b1, w2, b2, lin_w, lin_b, y_dram, out):
    NT = x.shape[0] // P
    NB = NT // BATCH
    ET = src_cols.shape[1]
    NG = ET // QUAD
    GAUSS = attr_t.shape[0]
    DUMP = x.shape[0]
    WINDOW = IN_FLIGHT - 1
    NBL = NB // XSLOTS
    assert NB % XSLOTS == 1 and NG % 2 == 1

    with ExitStack() as ctx:
        def sb(name, shape, dt=F32):
            return ctx.enter_context(nc.sbuf_tensor(name, shape, dt))

        def sem(name):
            return ctx.enter_context(nc.semaphore(name))

        ident = sb("ident", [P, P])
        ones = sb("ones", [P, P])
        before = sb("before", [P, (WINDOW + 1) * P])
        below = sb("below", [P, P])
        slot_row = sb("slot_row", [P, P])
        slot_row_i = sb("slot_row_i", [P, P], I32)
        dump4_i = sb("dump4_i", [P, QUAD], I32)
        dump4 = sb("dump4", [P, QUAD])
        edge_no_i = sb("edge_no_i", [P, ET], I32)
        edge_no = sb("edge_no", [P, ET])
        zero_rows = sb("zero_rows", [P, QUAD * D])
        w1_sb = sb("w1_sb", [GAUSS, D])
        w2_sb = sb("w2_sb", [P, D])
        lw_sb = sb("lw_sb", [P, D])
        b1_sb = sb("b1_sb", [P, 1])
        b2_sb = sb("b2_sb", [P, 1])
        lb3 = sb("lb3", [3, D])
        lb_res = sb("lb_res", [3, D])
        lb_part = sb("lb_part", [3, 3, D], BF16)
        lb_sel = sb("lb_sel", [3, QUAD, D], BF16)
        ones3 = sb("ones3", [3, P], BF16)
        src_i = sb("src_i", [P, ET], I32)
        src_f = sb("src_f", [P, WINDOW + ET])
        dst_i = sb("dst_i", [P, ET], I32)

        xs = sb("xs", [P, XSLOTS, BATCH, D])
        hn = sb("hn", [P, 2, BATCH, D])
        hT = sb("hT", [P, QUADS, QUAD * P])
        stat = sb("stat", [P, 2, BATCH, 6])
        chain = sb("chain", [P, 2, 8, BATCH])
        gx = sb("gx", [P, 2, QUAD, D])
        gidx = sb("gidx", [P, 2, QUAD], I32)
        xdst = sb("xdst", [P, ET, D])

        attr = sb("attr", [GAUSS, 2, QUAD * P])
        z_sb = sb("z_sb", [P, 2, QUAD * P])
        hTe = sb("hTe", [P, 2, QUAD * P])
        msg = sb("msg", [P, 2, QUAD * P])
        ysb = sb("ysb", [P, 2, QUAD, D])
        srcg = sb("srcg", [P, 2, WINDOW + QUAD])
        clash = sb("clash", [P, 2, QUAD])
        eqs = sb("eqs", [P, QUAD, (WINDOW + 1) * P], BF16)
        flags = sb("flags", [P, ET])
        off = sb("off", [P, 2, QUAD])
        sidx = sb("sidx", [P, 2, QUAD], I32)
        keys = sb("keys", [P, ET])

        top = sb("top", [P, TOP])
        pos = sb("pos", [P, 6, TOP])
        cnt = sb("cnt", [P, 8])
        slow_i = sb("slow_i", [P, 1], I32)
        onehot = sb("onehot", [P, TOP, P])
        lkey = sb("lkey", [P, 4])
        lidx = sb("lidx", [P, 1], I32)
        lsrc_i = sb("lsrc_i", [P, 1], I32)
        rsrc = sb("rsrc", [P, 4])
        same = sb("same", [P, P])
        ridx = sb("ridx", [P, 1], I32)
        ry = sb("ry", [P, D])
        rsum = sb("rsum", [P, D])

        ps = ctx.enter_context(nc.psum_tensor("ps", [P, 8, QUAD * P], F32))

        const_made = sem("const_made")
        ones_set = sem("ones_set")
        loaded = sem("loaded")
        prep = sem("prep")
        lin_b_ready = sem("lin_b_ready")
        x_loaded = [sem(f"x_loaded{s}") for s in range(XSLOTS)]
        out_stored = [sem(f"out_stored{s}") for s in range(XSLOTS)]
        dump_stored = sem("dump_stored")
        chain_step = sem("chain_step")
        var_ready = sem("var_ready")
        sd_ready = sem("sd_ready")
        rstd_ready = sem("rstd_ready")
        hn_by_dve = sem("hn_by_dve")
        hn_by_act = sem("hn_by_act")
        turned = [sem(f"turned{q}") for q in range(QUADS)]
        relu_done = [sem(f"relu_done{q}") for q in range(QUADS)]
        lin_done = [sem(f"lin_done{q}") for q in range(QUADS)]
        added = [sem(f"added{q}") for q in range(QUADS)]
        gidx_ready = sem("gidx_ready")
        gathered = [sem(f"gathered{s}") for s in range(2)]
        xdst_ready = sem("xdst_ready")

        attr_loaded = [sem(f"attr_loaded{s}") for s in range(2)]
        e_chain = sem("e_chain")
        e_var = sem("e_var")
        e_sd = sem("e_sd")
        e_rstd = sem("e_rstd")
        e_hn = sem("e_hn")
        e_turned = sem("e_turned")
        e_hT = sem("e_hT")
        z_done = sem("z_done")
        z_relu = sem("z_relu")
        w_done = sem("w_done")
        msg_ready = sem("msg_ready")
        y_done = sem("y_done")
        y_ready = sem("y_ready")
        y_stored = [sem(f"y_stored{s}") for s in range(2)]
        srcg_ready = sem("srcg_ready")
        rows_ready = sem("rows_ready")
        clash_ready = sem("clash_ready")
        sidx_step = sem("sidx_step")
        sidx_ready = sem("sidx_ready")
        scattered = [sem(f"scattered{k}") for k in range(QUAD)]

        pack_step = sem("pack_step")
        counts_ready = sem("counts_ready")
        base_ready = sem("base_ready")
        onehot_ready = sem("onehot_ready")
        list_ready = sem("list_ready")
        lidx_ready = sem("lidx_ready")
        l_gathered = sem("l_gathered")
        slow_ready = sem("slow_ready")
        r_src = sem("r_src")
        r_row = sem("r_row")
        r_step = sem("r_step")
        r_same = sem("r_same")
        r_sum = sem("r_sum")
        r_ready = sem("r_ready")
        r_scattered = sem("r_scattered")
        r_y = sem("r_y")

        x_by_part = x.rearrange("(p t) f -> p (t f)", t=NT)
        out_by_part = out[0:DUMP, :].rearrange("(p t) f -> p (t f)", t=NT)
        y_by_group = y_dram.rearrange("(g t p) f -> g p t f", t=QUAD, p=P)
        BL = BATCH * D

        block = ctx.enter_context(nc.Block())

        N_CONST = 6
        N_LOADS = 8
        PREP = 16 * N_LOADS

        @block.sync
        def _(sp):
            sp.dma_start(dst_i[:, :], dst_cols).then_inc(loaded, 16)

            def load(i, s):
                b = i * XSLOTS + s
                sp.dma_start(xs[:, s, :, :].rearrange("p t f -> p (t f)"),
                             x_by_part[:, bass.ts(b, BL)]).then_inc(x_loaded[s], 16)

            def store(i, s):
                b = i * XSLOTS + s
                sp.wait_ge(added[QUADS - 1], b + 1)
                sp.dma_start(out_by_part[:, bass.ts(b, BL)],
                             xs[:, s, :, :].rearrange("p t f -> p (t f)")).then_inc(out_stored[s], 16)

            load(0, 0)
            sp.dma_start(lw_sb[:, :], lin_w).then_inc(loaded, 16)
            sp.dma_start(lb3[:, :], lin_b.to_broadcast([3, D])).then_inc(loaded, 16)
            load(0, 1)
            load(0, 2)
            sp.dma_start(src_i[:, :], src_cols).then_inc(loaded, 16)
            sp.dma_start(w1_sb[:, :], w1).then_inc(loaded, 16)
            sp.dma_start(w2_sb[:, :], w2).then_inc(loaded, 16)
            sp.dma_start(b1_sb[:, :], b1).then_inc(loaded, 16)
            sp.dma_start(b2_sb[:, :], b2).then_inc(loaded, 16)
            sp.wait_ge(ones_set, 1)
            sp.dma_start(out[DUMP:DUMP + QUAD * P, :].rearrange("(p t) f -> p (t f)", t=QUAD),
                         zero_rows[:, :]).then_inc(dump_stored, 16)

            def step(i, s, more):
                store(i, s)
                if more:
                    before_s = (s + XSLOTS - 1) % XSLOTS
                    if s or not isinstance(i, int) or i:
                        sp.wait_ge(out_stored[before_s], 16 * (i + 1 if s else i))
                    load(i + 1 if s else i, before_s)

            step(0, 0, True)
            with sp.Fori(0, NBL - 1) as i:
                for b in range(1, XSLOTS + 1):
                    step(i + b // XSLOTS, b % XSLOTS, True)
            for b in range((NBL - 1) * XSLOTS + 1, NB):
                step(b // XSLOTS, b % XSLOTS, b + XSLOTS - 1 < NB)

            def load_attr(g, s):
                sp.dma_start(attr[:, s, :], attr_t[:, bass.ts(g, QUAD * P)]).then_inc(attr_loaded[s], 16)

            def edge_step(g, s, more):
                if more:
                    sp.wait_ge(z_done, g + 1)
                    load_attr(g + 2, s)
                sp.wait_ge(y_ready, g + 1)
                sp.dma_start(y_by_group[g], ysb[:, s, :, :]).then_inc(y_stored[s], 16)

            load_attr(0, 0)
            load_attr(1, 1)
            with sp.Fori(0, NG // 2 - 1) as i:
                for s in range(2):
                    edge_step(i * 2 + s, s, True)
            for g in range(NG - 3, NG):
                edge_step(g, g % 2, g + 2 < NG)
            for s in range(2):
                sp.wait_ge(y_stored[s], 16 * ((NG + 1 - s) // 2))

            sp.wait_ge(slow_ready, 1)
            slow = sp.value_load(slow_i[0:1, 0:1], min_val=0, max_val=1)
            with sp.If(slow == 1):
                with sp.Fori(0, ET) as t:
                    sp.wait_ge(r_scattered, 16 * (t + 1))
                    sp.dma_start(ry[:, :], y_dram[bass.ts(t, P), :]).then_inc(r_y, 16)

        @block.gpsimd
        def _(pool):
            nc.gpsimd.memset(ident[:, :], 0.0).then_inc(const_made, 1)
            pool.wait_ge(const_made, 1)
            nc.gpsimd.affine_select(out=ident[:, :], in_=ident[:, :], compare_op=ALU.not_equal, fill=1.0,
                                    base=0, pattern=[[-1, P]], channel_multiplier=1).then_inc(const_made, 1)
            nc.gpsimd.iota(slot_row_i[:, :], [[1, P]], base=0, channel_multiplier=0).then_inc(const_made, 1)
            nc.gpsimd.iota(dump4_i[:, :], [[P, QUAD]], base=DUMP, channel_multiplier=1).then_inc(const_made, 1)
            nc.gpsimd.iota(edge_no_i[:, :], [[P, ET]], base=1, channel_multiplier=1).then_inc(const_made, 1)
            pool.wait_ge(ones_set, 2)
            nc.gpsimd.affine_select(out=before[:, WINDOW * P:], in_=before[:, WINDOW * P:],
                                    compare_op=ALU.is_gt, fill=0.0, base=0, pattern=[[-1, P]],
                                    channel_multiplier=1)
            nc.gpsimd.affine_select(out=below[:, :], in_=below[:, :], compare_op=ALU.is_gt, fill=0.0,
                                    base=0, pattern=[[1, P]], channel_multiplier=-1).then_inc(const_made, 1)
            pool.wait_ge(loaded, PREP)

            group_no = pool.alloc_register("group_no")
            landed_before = pool.alloc_register("landed_before")
            landed_now = pool.alloc_register("landed_now")
            round_no = pool.alloc_register("round_no")
            pool.reg_mov(group_no, 0)

            def gather(g, s, n):
                pool.reg_add(group_no, group_no, 1)
                nc.gpsimd.tensor_copy(gidx[:, s, :], dst_i[:, bass.ts(g, QUAD)]).then_inc(gidx_ready, 1)
                pool.wait_ge(loaded, PREP)
                pool.wait_ge(gidx_ready, group_no)
                for k in range(QUAD):
                    nc.gpsimd.indirect_dma_start(
                        gx[:, s, k, :], None, x,
                        bass.IndirectOffsetOnAxis(ap=gidx[:, s, k:k + 1], axis=0)).then_inc(gathered[s], 16)

            def put(g, s, n):
                pool.wait_ge(gathered[s], 16 * QUAD * (n + 1))
                nc.gpsimd.tensor_copy(xdst[:, bass.ts(g, QUAD), :].rearrange("p t f -> p (t f)"),
                                      gx[:, s, :, :].rearrange("p t f -> p (t f)")).then_inc(xdst_ready, 1)
                pool.wait_ge(xdst_ready, g + 1)

            gather(0, 0, 0)
            with pool.Fori(0, NG // 2) as i:
                gather(i * 2 + 1, 1, i)
                put(i * 2, 0, i)
                gather(i * 2 + 2, 0, i + 1)
                put(i * 2 + 1, 1, i)
            put(NG - 1, 0, NG // 2)

            for s in range(XSLOTS):
                pool.wait_ge(out_stored[s], 16 * ((NB - s + XSLOTS - 1) // XSLOTS))
            pool.wait_ge(dump_stored, 16)

            def scatter(s, first):
                pool.reg_add(group_no, group_no, 1)
                pool.reg_mov(landed_before, landed_now)
                pool.reg_add(landed_now, landed_now, 16)
                pool.wait_ge(dump_stored, 16)
                pool.wait_ge(y_ready, group_no)
                pool.wait_ge(sidx_ready, group_no)
                for k in range(QUAD):
                    pool.wait_ge(dump_stored, 16)
                    if k < QUAD - 1 and not first:
                        pool.wait_ge(scattered[k + 1], landed_before)
                    elif k == QUAD - 1:
                        pool.wait_ge(scattered[0], landed_now)
                    nc.gpsimd.indirect_dma_start(
                        out, bass.IndirectOffsetOnAxis(ap=sidx[:, s, k:k + 1], axis=0),
                        ysb[:, s, k, :], None, compute_op=ALU.add).then_inc(scattered[k], 16)

            pool.reg_mov(group_no, 0)
            pool.reg_mov(landed_now, 0)
            scatter(0, True)
            with pool.Fori(0, NG // 2) as i:
                for s in (1, 0):
                    scatter(s, False)
            for k in range(QUAD):
                pool.wait_ge(scattered[k], 16 * NG)

            pool.wait_ge(lidx_ready, 1)
            for s in range(2):
                pool.wait_ge(y_stored[s], 16 * ((NG + 1 - s) // 2))
            nc.gpsimd.indirect_dma_start(
                lsrc_i[:, :], None, src_rows,
                bass.IndirectOffsetOnAxis(ap=lidx[:, :], axis=0)).then_inc(l_gathered, 16)
            nc.gpsimd.indirect_dma_start(
                ry[:, :], None, y_dram,
                bass.IndirectOffsetOnAxis(ap=lidx[:, :], axis=0)).then_inc(l_gathered, 16)

            def add_sums(n):
                pool.reg_add(round_no, round_no, 1)
                pool.wait_ge(dump_stored, 16)
                pool.wait_ge(r_ready, round_no)
                nc.gpsimd.indirect_dma_start(
                    out, bass.IndirectOffsetOnAxis(ap=ridx[:, :], axis=0),
                    rsum[:, :], None, compute_op=ALU.add).then_inc(r_scattered, 16)
                pool.wait_ge(r_scattered, 16 * (n + 1))

            pool.reg_mov(round_no, 0)
            add_sums(0)
            slow = pool.value_load(slow_i[0:1, 0:1], min_val=0, max_val=1)
            with pool.If(slow == 1):
                with pool.Fori(0, ET) as t:
                    add_sums(t + 1)

        @block.tensor
        def _(pe):
            pe.wait_ge(const_made, 2)
            pe.wait_ge(lin_b_ready, 1)
            pe.wait_ge(loaded, PREP)

            def turn(b, h, q):
                pe.wait_ge(hn_by_dve, b * QUADS + q + 1)
                pe.wait_ge(hn_by_act, b * QUADS + q + 1)
                for k in range(QUAD):
                    last = nc.tensor.transpose(ps[:, q, k * P:(k + 1) * P], hn[:, h, q * QUAD + k, :], ident[:, :])
                last.then_inc(turned[q], 1)

            def lin(b, q):
                pe.wait_ge(relu_done[q], b + 1)
                if not isinstance(b, int) or b:
                    pe.wait_ge(added[q], b)
                for k in range(QUAD):
                    nc.tensor.matmul(ps[:, QUADS + q, k * P:(k + 1) * P], hT[:, q, k * P:(k + 1) * P], lw_sb[:, :],
                                     start=(k == 0), stop=False, skip_group_check=True)
                nc.tensor.matmul(ps[:, QUADS + q, :], ones3[:, :], lb_sel[:, :, :].rearrange("p t f -> p (t f)"),
                                 start=False, stop=True, skip_group_check=True).then_inc(lin_done[q], 1)

            def node_batch(i, s):
                b = i * XSLOTS + s
                turn(b, s % 2, 0)
                for q in range(1, QUADS):
                    turn(b, s % 2, q)
                    lin(b, q - 1)
                lin(b, QUADS - 1)

            node_batch(0, 0)
            with pe.Fori(0, NBL) as i:
                for b in range(1, XSLOTS + 1):
                    node_batch(i + b // XSLOTS, b % XSLOTS)

            def g0(g):
                return not isinstance(g, int) or g > 0

            def z(g, s, n):
                pe.wait_ge(attr_loaded[s], 16 * (n + 1))
                if g0(g):
                    pe.wait_ge(z_relu, g)
                nc.tensor.matmul(ps[:, 0, :], w1_sb[:, :], attr[:, s, :], start=True, stop=True).then_inc(z_done, 1)

            def edge_group(g, s, n, more):
                pe.wait_ge(e_hn, g + 1)
                if g0(g):
                    pe.wait_ge(e_hT, g)
                for k in range(QUAD):
                    last = nc.tensor.transpose(ps[:, 2, k * P:(k + 1) * P], hn[:, s, k, :], ident[:, :])
                last.then_inc(e_turned, 1)
                pe.wait_ge(z_relu, g + 1)
                if g0(g):
                    pe.wait_ge(msg_ready, g)
                nc.tensor.matmul(ps[:, 1, :], w2_sb[:, :], z_sb[:, s, :], start=True, stop=True).then_inc(w_done, 1)
                pe.wait_ge(srcg_ready, g + 1)
                if g0(g):
                    pe.wait_ge(clash_ready, g)
                for k in range(WINDOW + QUAD):
                    last = nc.tensor.transpose(ps[:, 4 + 2 * s + k // QUAD, (k % QUAD) * P:(k % QUAD + 1) * P],
                                               srcg[:, s, k:k + 1].to_broadcast([P, P]), ident[:, :])
                last.then_inc(rows_ready, 1)
                if more:
                    z(g + 1, 1 - s, n + s)
                pe.wait_ge(msg_ready, g + 1)
                if g0(g):
                    pe.wait_ge(y_ready, g)
                for k in range(QUAD):
                    last = nc.tensor.matmul(ps[:, 3, k * P:(k + 1) * P], msg[:, s, k * P:(k + 1) * P], lw_sb[:, :],
                                            start=True, stop=True, skip_group_check=True)
                last.then_inc(y_done, 1)

            z(0, 0, 0)
            edge_group(0, 0, 0, True)
            with pe.Fori(0, NG // 2 - 1) as i:
                edge_group(i * 2 + 1, 1, i, True)
                edge_group(i * 2 + 2, 0, i + 1, True)
            edge_group(NG - 2, 1, NG // 2 - 1, True)
            edge_group(NG - 1, 0, NG // 2, False)

            pe.wait_ge(counts_ready, 1)
            nc.tensor.matmul(ps[:, 0, 0:1], below[:, :], cnt[:, 0:1], start=True, stop=True)
            nc.tensor.matmul(ps[:, 0, 2:4], ones[:, :], cnt[:, 0:2], start=True, stop=True).then_inc(base_ready, 1)
            pe.wait_ge(onehot_ready, 1)
            for k in range(TOP):
                last = nc.tensor.matmul(ps[:, 1, 0:1], onehot[:, k, :], top[:, k:k + 1],
                                        start=(k == 0), stop=(k == TOP - 1))
            last.then_inc(list_ready, 1)

            def sums(n):
                pe.wait_ge(r_src, n + 1)
                nc.tensor.transpose(ps[:, 2, 0:P], rsrc[:, 0:1].to_broadcast([P, P]), ident[:, :]).then_inc(r_row, 1)
                pe.wait_ge(r_same, n + 1)
                nc.tensor.matmul(ps[:, 3, 0:D], same[:, :], ry[:, :], start=True, stop=True).then_inc(r_sum, 1)

            pe.wait_ge(l_gathered, 32)
            sums(0)
            slow = pe.value_load(slow_i[0:1, 0:1], min_val=0, max_val=1)
            with pe.If(slow == 1):
                with pe.Fori(0, ET) as t:
                    pe.wait_ge(r_y, 16 * (t + 1))
                    sums(t + 1)

        @block.scalar
        def _(act):
            act.wait_ge(loaded, PREP)

            def relu_quad(b, q):
                act.wait_ge(turned[q], b + 1)
                nc.scalar.activation(hT[:, q, :], ps[:, q, :], ACT.Relu).then_inc(relu_done[q], 1)

            def root(b, h):
                act.wait_ge(var_ready, b + 1)
                nc.scalar.activation(chain[:, h, 5, :], chain[:, h, 4, :], ACT.Sqrt).then_inc(sd_ready, 1)

            def norm(b, s):
                act.wait_ge(x_loaded[s % XSLOTS], 16)
                act.wait_ge(rstd_ready, b + 1)
                for q in range(QUADS):
                    for k in range(ACT_NORM):
                        t = q * QUAD + k
                        last = nc.scalar.activation(hn[:, s % 2, t, :], xs[:, s, t, :], ACT.Identity,
                                                    bias=chain[:, s % 2, 7, t:t + 1], scale=chain[:, s % 2, 6, t:t + 1])
                    last.then_inc(hn_by_act, 1)

            root(0, 0)
            norm(0, 0)

            def node_step(i, s):
                b = i * XSLOTS + s
                for q in range(QUADS):
                    relu_quad(b, q)
                    if q == 2:
                        root(b + 1, (s + 1) % 2)
                norm(b + 1, (s + 1) % XSLOTS)

            with act.Fori(0, NBL) as i:
                for s in range(XSLOTS):
                    node_step(i, s)
            for q in range(QUADS):
                relu_quad(NB - 1, q)

            def relu_z(g, s):
                act.wait_ge(z_done, g + 1)
                nc.scalar.activation(z_sb[:, s, :], ps[:, 0, :], ACT.Relu, bias=b1_sb[:, 0:1]).then_inc(z_relu, 1)

            def e_root(g, s):
                act.wait_ge(e_var, g + 1)
                nc.scalar.activation(chain[:, s, 5, 0:QUAD], chain[:, s, 4, 0:QUAD], ACT.Sqrt).then_inc(e_sd, 1)

            def e_norm(g, s):
                act.wait_ge(e_rstd, g + 1)
                for k in range(QUAD):
                    last = nc.scalar.activation(hn[:, s, k, :], xdst[:, bass.ds(g * QUAD + k, 1), :].rearrange("p t f -> p (t f)"), ACT.Identity,
                                                bias=chain[:, s, 7, k:k + 1], scale=chain[:, s, 6, k:k + 1])
                last.then_inc(e_hn, 1)

            relu_z(0, 0)
            e_root(0, 0)
            e_norm(0, 0)
            for g in range(2):
                act.wait_ge(e_turned, g + 1)
                nc.scalar.activation(hTe[:, g, :], ps[:, 2, :], ACT.Relu).then_inc(e_hT, 1)
                relu_z(g + 1, 1 - g)
                e_root(g + 1, 1 - g)
                e_norm(g + 1, 1 - g)
                act.wait_ge(y_done, g + 1)
                nc.scalar.activation(ysb[:, g, :, :].rearrange("p t f -> p (t f)"), ps[:, 3, :],
                                     ACT.Copy).then_inc(y_ready, 1)

            def edge_step(g, s, n, more):
                act.wait_ge(e_turned, g + 1)
                nc.scalar.activation(hTe[:, s, :], ps[:, 2, :], ACT.Relu).then_inc(e_hT, 1)
                if more:
                    relu_z(g + 1, 1 - s)
                    e_root(g + 1, 1 - s)
                    e_norm(g + 1, 1 - s)
                act.wait_ge(y_done, g + 1)
                for k in range(QUAD):
                    act.wait_ge(scattered[k], 16 * (g - 1))
                act.wait_ge(y_stored[s], 16 * n)
                nc.scalar.activation(ysb[:, s, :, :].rearrange("p t f -> p (t f)"), ps[:, 3, :],
                                     ACT.Copy).then_inc(y_ready, 1)

            with act.Fori(1, NG // 2) as i:
                for s in range(2):
                    edge_step(i * 2 + s, s, i, True)
            edge_step(NG - 1, 0, NG // 2, False)

        @block.vector
        def _(dve):
            nc.vector.memset(zero_rows[:, :], 0.0).then_inc(ones_set, 1)
            nc.vector.memset(ones[:, :], 1.0)
            nc.vector.memset(below[:, :], 1.0)
            nc.vector.memset(before[:, :], 1.0).then_inc(ones_set, 1)
            nc.vector.memset(ones3[:, :], 1.0)
            nc.vector.memset(src_f[:, 0:WINDOW], -1.0)
            done = [0]

            def then(ins):
                done[0] += 1
                ins.then_inc(prep, 1)
                dve.wait_ge(prep, done[0])

            dve.wait_ge(loaded, PREP)
            dve.wait_ge(const_made, 5)
            nc.vector.tensor_copy(src_f[:, WINDOW:], src_i[:, :])
            nc.vector.tensor_copy(slot_row[:, :], slot_row_i[:, :])
            nc.vector.tensor_copy(dump4[:, :], dump4_i[:, :])
            nc.vector.tensor_copy(edge_no[:, :], edge_no_i[:, :])
            then(nc.vector.tensor_copy(lb_part[:, 0, :], lb3[:, :]))
            then(nc.vector.tensor_tensor(lb_res[:, :], lb3[:, :], lb_part[:, 0, :], ALU.subtract))
            then(nc.vector.tensor_copy(lb_part[:, 1, :], lb_res[:, :]))
            then(nc.vector.tensor_tensor(lb_res[:, :], lb_res[:, :], lb_part[:, 1, :], ALU.subtract))
            then(nc.vector.tensor_copy(lb_part[:, 2, :], lb_res[:, :]))
            then(nc.vector.tensor_scalar(lb_sel[:, 0, :], lb_part[:, 0, :], ident[0:3, 0:1], None, ALU.mult))
            for k in (1, 2):
                then(nc.vector.scalar_tensor_tensor(out=lb_sel[:, 0, :], in0=lb_part[:, k, :], scalar=ident[0:3, k:k + 1],
                                                    in1=lb_sel[:, 0, :], op0=ALU.mult, op1=ALU.add))
            for k in range(1, QUAD):
                then(nc.vector.tensor_copy(lb_sel[:, k, :], lb_sel[:, 0, :]))
            dve.sem_inc(lin_b_ready, 1)

            STEPS = 10

            def stats(tiles, h, sem_, b):
                for t, tile in enumerate(tiles):
                    last = nc.vector.bn_stats(stat[:, h, t, :], tile)
                last.then_inc(sem_, 1)

            def moments(n, h, sem_, var_sem, b):
                def after(k):
                    dve.wait_ge(sem_, b * STEPS + k)
                st = stat[:, h, 0:n, :]
                c = lambda r: chain[:, h, r, 0:n]
                after(1)
                nc.vector.tensor_tensor(c(1), st[:, :, 1], st[:, :, 4], ALU.subtract).then_inc(sem_, 1)
                nc.vector.tensor_tensor(c(2), st[:, :, 2], st[:, :, 5], ALU.add).then_inc(sem_, 1)
                nc.vector.tensor_tensor(c(0), st[:, :, 1], st[:, :, 4], ALU.add).then_inc(sem_, 1)
                after(2)
                nc.vector.scalar_tensor_tensor(out=c(3), in0=c(1), scalar=float(D // 4), in1=c(1),
                                               op0=ALU.mult, op1=ALU.mult).then_inc(sem_, 1)
                after(5)
                nc.vector.tensor_tensor(c(1), c(2), c(3), ALU.add).then_inc(sem_, 1)
                after(6)
                nc.vector.tensor_scalar(c(4), c(1), 1.0 / D, EPS, ALU.mult, ALU.add).then_inc(var_sem, 1)

            def rstd(n, h, sem_, var_sem, sd_sem, ready_sem, b):
                def after(k):
                    dve.wait_ge(sem_, b * STEPS + k)
                c = lambda r: chain[:, h, r, 0:n]
                dve.wait_ge(sd_sem, b + 1)
                nc.vector.reciprocal(c(1), c(5)).then_inc(sem_, 1)
                after(7)
                nc.vector.tensor_tensor(c(2), c(1), c(1), ALU.mult).then_inc(sem_, 1)
                after(8)
                nc.vector.scalar_tensor_tensor(out=c(3), in0=c(2), scalar=-0.5, in1=c(4),
                                               op0=ALU.mult, op1=ALU.mult).then_inc(sem_, 1)
                after(9)
                nc.vector.scalar_tensor_tensor(out=c(6), in0=c(3), scalar=1.5, in1=c(1),
                                               op0=ALU.add, op1=ALU.mult).then_inc(sem_, 1)
                after(10)
                nc.vector.scalar_tensor_tensor(out=c(7), in0=c(0), scalar=-0.5, in1=c(6),
                                               op0=ALU.mult, op1=ALU.mult).then_inc(ready_sem, 1)
                dve.wait_ge(ready_sem, b + 1)

            def node_stats(i, s):
                dve.wait_ge(x_loaded[s], 16 * (i + 1))
                stats([xs[:, s, t, :] for t in range(BATCH)], s % 2, chain_step, i * XSLOTS + s)

            def add_quad(b, s, q):
                dve.wait_ge(lin_done[q], b + 1)
                x_quad = xs[:, s, q * QUAD:(q + 1) * QUAD, :].rearrange("p t f -> p (t f)")
                nc.vector.tensor_tensor(x_quad, ps[:, QUADS + q, :], x_quad, ALU.add).then_inc(added[q], 1)

            def norm(b, s):
                for q in range(QUADS):
                    for k in range(ACT_NORM, QUAD):
                        t = q * QUAD + k
                        last = nc.vector.tensor_scalar(hn[:, s % 2, t, :], xs[:, s, t, :], chain[:, s % 2, 6, t:t + 1],
                                                       chain[:, s % 2, 7, t:t + 1], ALU.mult, ALU.add)
                    last.then_inc(hn_by_dve, 1)

            node_stats(0, 0)
            moments(BATCH, 0, chain_step, var_ready, 0)
            rstd(BATCH, 0, chain_step, var_ready, sd_ready, rstd_ready, 0)
            norm(0, 0)

            def node_step(i, s):
                b = i * XSLOTS + s
                h = (s + 1) % 2
                node_stats(i if s + 1 < XSLOTS else i + 1, (s + 1) % XSLOTS)
                add_quad(b, s, 0)
                moments(BATCH, h, chain_step, var_ready, b + 1)
                add_quad(b, s, 1)
                rstd(BATCH, h, chain_step, var_ready, sd_ready, rstd_ready, b + 1)
                norm(b + 1, (s + 1) % XSLOTS)
                add_quad(b, s, 2)
                add_quad(b, s, 3)

            with dve.Fori(0, NBL) as i:
                for s in range(XSLOTS):
                    node_step(i, s)
            for q in range(QUADS):
                add_quad(NB - 1, 0, q)

            def e_stats(g, s):
                dve.wait_ge(xdst_ready, g + 1)
                stats([xdst[:, bass.ds(g * QUAD + k, 1), :].rearrange("p t f -> p (t f)") for k in range(QUAD)], s, e_chain, g)

            def e_prepare(g, s):
                moments(QUAD, s, e_chain, e_var, g)

            def e_finish(g, s):
                rstd(QUAD, s, e_chain, e_var, e_sd, e_rstd, g)

            def sources(g, s):
                nc.vector.tensor_copy(srcg[:, s, :], src_f[:, bass.ds(g * QUAD, WINDOW + QUAD)]).then_inc(srcg_ready, 1)

            def clashes(g, s):
                dve.wait_ge(rows_ready, g + 1)
                rows = ps[:, 4 + 2 * s:6 + 2 * s, :].rearrange("p b c -> p (b c)")
                for k in range(QUAD):
                    last = nc.vector.scalar_tensor_tensor(
                        out=eqs[:, k, :], in0=rows[:, k * P:(k + WINDOW + 1) * P], scalar=srcg[:, s, WINDOW + k:WINDOW + k + 1],
                        in1=before[:, :], op0=ALU.is_equal, op1=ALU.mult, accum_out=clash[:, s, k:k + 1])
                last.then_inc(clash_ready, 1)

            def targets(g, s):
                dve.wait_ge(clash_ready, g + 1)
                own = srcg[:, s, WINDOW:]
                nc.vector.tensor_tensor(off[:, s, :], dump4[:, :], own, ALU.subtract).then_inc(sidx_step, 1)
                nc.vector.scalar_tensor_tensor(out=keys[:, bass.ds(g * QUAD, QUAD)], in0=clash[:, s, :], scalar=1.0,
                                               in1=edge_no[:, bass.ds(g * QUAD, QUAD)],
                                               op0=ALU.min, op1=ALU.mult).then_inc(sidx_step, 1)
                dve.wait_ge(sidx_step, g * 3 + 1)
                nc.vector.scalar_tensor_tensor(out=off[:, s, :], in0=clash[:, s, :], scalar=1.0, in1=off[:, s, :],
                                               op0=ALU.min, op1=ALU.mult).then_inc(sidx_step, 1)
                dve.wait_ge(sidx_step, g * 3 + 3)
                nc.vector.tensor_tensor(sidx[:, s, :], off[:, s, :], own, ALU.add).then_inc(sidx_ready, 1)

            def message(g, s):
                dve.wait_ge(w_done, g + 1)
                dve.wait_ge(e_hT, g + 1)
                dve.wait_ge(y_done, g)
                nc.vector.scalar_tensor_tensor(out=msg[:, s, :], in0=ps[:, 1, :], scalar=b2_sb[:, 0:1], in1=hTe[:, s, :],
                                               op0=ALU.add, op1=ALU.mult).then_inc(msg_ready, 1)

            def edge_step(g, s, more, older):
                if more:
                    e_stats(g + 1, 1 - s)
                    dve.wait_ge(sidx_ready, g)
                    sources(g + 1, 1 - s)
                    e_prepare(g + 1, 1 - s)
                clashes(g, s)
                message(g, s)
                if more:
                    e_finish(g + 1, 1 - s)
                if older:
                    for k in range(QUAD):
                        dve.wait_ge(scattered[k], 16 * (g - 1))
                targets(g, s)

            e_stats(0, 0)
            sources(0, 0)
            e_prepare(0, 0)
            e_finish(0, 0)
            for g in range(2):
                edge_step(g, g, True, False)
            with dve.Fori(1, NG // 2) as i:
                for s in range(2):
                    edge_step(i * 2 + s, s, True, True)
            edge_step(NG - 1, 0, False, True)

            packed = [0]

            def link(ins):
                packed[0] += 1
                ins.then_inc(pack_step, 1)
                dve.wait_ge(pack_step, packed[0])

            dve.wait_ge(sidx_step, 3 * NG)
            link(nc.vector.max(top[:, :], keys[:, :]))
            link(nc.vector.tensor_scalar(pos[:, 0, :], top[:, :], 0.0, None, ALU.is_gt))
            link(nc.vector.tensor_reduce(cnt[:, 0:1], pos[:, 0, :], AX_X, ALU.add))
            link(nc.vector.tensor_scalar(flags[:, :], keys[:, :], 0.0, None, ALU.is_gt))
            nc.vector.tensor_reduce(cnt[:, 1:2], flags[:, :], AX_X, ALU.add).then_inc(counts_ready, 1)
            dve.wait_ge(base_ready, 1)
            link(nc.vector.tensor_copy(cnt[:, 2:3], ps[:, 0, 0:1]))
            link(nc.vector.tensor_copy(cnt[:, 3:5], ps[:, 0, 2:4]))
            link(nc.vector.tensor_tensor(cnt[:, 5:6], cnt[:, 4:5], cnt[:, 3:4], ALU.is_gt))
            link(nc.vector.tensor_scalar(cnt[:, 6:7], cnt[:, 4:5], float(P), None, ALU.is_gt))
            link(nc.vector.tensor_tensor(cnt[:, 5:6], cnt[:, 5:6], cnt[:, 6:7], ALU.max))
            link(nc.vector.tensor_copy(slow_i[:, :], cnt[:, 5:6]))
            link(nc.vector.tensor_scalar(cnt[:, 6:7], cnt[:, 5:6], -1.0, 1.0, ALU.mult, ALU.add))
            link(nc.vector.tensor_scalar(pos[:, 1, :], pos[:, 0, :], cnt[:, 6:7], None, ALU.mult))
            link(nc.vector.tensor_scalar(pos[:, 2, :], slot_row[:, 0:TOP], cnt[:, 2:3], 1.0, ALU.add, ALU.add))
            link(nc.vector.tensor_tensor(pos[:, 3, :], pos[:, 2, :], pos[:, 1, :], ALU.mult))
            link(nc.vector.tensor_scalar(pos[:, 4, :], pos[:, 3, :], 1.0, None, ALU.subtract))
            for k in range(TOP):
                last = nc.vector.tensor_scalar(onehot[:, k, :], slot_row[:, :], pos[:, 4, k:k + 1], None, ALU.is_equal)
            last.then_inc(onehot_ready, 1)
            dve.wait_ge(list_ready, 1)
            link(nc.vector.tensor_copy(lkey[:, 0:1], ps[:, 1, 0:1]))
            link(nc.vector.tensor_scalar(lkey[:, 1:2], lkey[:, 0:1], 1.0, None, ALU.min))
            link(nc.vector.tensor_tensor(lkey[:, 2:3], lkey[:, 0:1], lkey[:, 1:2], ALU.subtract))
            nc.vector.tensor_copy(lidx[:, :], lkey[:, 2:3]).then_inc(lidx_ready, 1)
            dve.wait_ge(l_gathered, 32)
            dump = dump4[:, QUAD - 1:QUAD]

            def pick(source, taken, n, wait):
                wait(nc.vector.tensor_tensor(rsrc[:, 1:2], source, dump, ALU.subtract))
                wait(nc.vector.tensor_tensor(rsrc[:, 2:3], rsrc[:, 1:2], taken, ALU.mult))
                nc.vector.tensor_tensor(rsrc[:, 0:1], rsrc[:, 2:3], dump, ALU.add).then_inc(r_src, 1)

            def sums(n, wait):
                dve.wait_ge(r_src, n + 1)
                dve.wait_ge(r_row, n + 1)
                nc.vector.tensor_scalar(same[:, :], ps[:, 2, 0:P], rsrc[:, 0:1], None, ALU.is_equal).then_inc(r_same, 1)
                wait(nc.vector.scalar_tensor_tensor(out=eqs[:, 0, 0:P], in0=ps[:, 2, 0:P], scalar=rsrc[:, 0:1],
                                                    in1=before[:, WINDOW * P:], op0=ALU.is_equal, op1=ALU.mult,
                                                    accum_out=lkey[:, 3:4]))
                wait(nc.vector.tensor_tensor(rsrc[:, 1:2], dump, rsrc[:, 0:1], ALU.subtract))
                wait(nc.vector.scalar_tensor_tensor(out=rsrc[:, 2:3], in0=lkey[:, 3:4], scalar=1.0, in1=rsrc[:, 1:2],
                                                    op0=ALU.min, op1=ALU.mult))
                wait(nc.vector.tensor_tensor(ridx[:, :], rsrc[:, 2:3], rsrc[:, 0:1], ALU.add))
                dve.wait_ge(r_sum, n + 1)
                nc.vector.tensor_copy(rsum[:, :], ps[:, 3, 0:D]).then_inc(r_ready, 1)

            link(nc.vector.tensor_copy(rsrc[:, 3:4], lsrc_i[:, :]))
            pick(rsrc[:, 3:4], lkey[:, 1:2], 0, link)
            sums(0, link)
            dve.sem_inc(slow_ready, 1)

            slow = dve.value_load(slow_i[0:1, 0:1], min_val=0, max_val=1)
            with dve.If(slow == 1):
                with dve.Fori(0, ET) as t:
                    n = t + 1
                    k = [0]

                    def turn(ins):
                        k[0] += 1
                        ins.then_inc(r_step, 1)
                        dve.wait_ge(r_step, t * 8 + k[0])

                    dve.wait_ge(r_scattered, 16 * n)
                    turn(nc.vector.tensor_scalar(lkey[:, 1:2], keys[:, bass.ds(t, 1)], 1.0, None, ALU.min))
                    turn(nc.vector.tensor_copy(rsrc[:, 3:4], src_f[:, bass.ds(t + WINDOW, 1)]))
                    pick(rsrc[:, 3:4], lkey[:, 1:2], n, turn)
                    sums(n, turn)


_INS = ["x", "src_cols", "src_rows", "dst_cols", "attr_t", "w1", "b1", "w2", "b2", "lin_w", "lin_b"]


def kernel(x, src, dst, edge_attr_50, edge_weight, L0_gnn_mlp_w1, L0_gnn_mlp_b1, L0_gnn_mlp_w2, L0_gnn_mlp_b2,
           L0_gnn_lin_w, L0_gnn_lin_b):
    import numpy as np
    import concourse.bacc as bacc
    from concourse.bass_utils import run_bass_kernel_spmd

    nodes, feats = x.shape
    edges = src.shape[0]
    nt, et = node_tiles(nodes), edge_tiles(edges)

    def padded(a, rows, fill):
        full = np.empty((rows,) + a.shape[1:], a.dtype)
        full[:a.shape[0]] = a
        full[a.shape[0]:] = fill
        return full

    pads = np.arange(edges, et * P)
    dump_rows = (nt * P + (pads // P % QUAD) * P + pads % P).astype(np.int32)
    src_p = padded(np.asarray(src), et * P, dump_rows)
    dst_p = padded(np.asarray(dst), et * P, 0)
    attr_p = padded(np.asarray(edge_attr_50), et * P, 0)
    arrays = {
        "x": padded(np.asarray(x), nt * P, 0),
        "src_cols": np.ascontiguousarray(src_p.reshape(et, P).T),
        "src_rows": src_p.reshape(et * P, 1),
        "dst_cols": np.ascontiguousarray(dst_p.reshape(et, P).T),
        "attr_t": np.ascontiguousarray(attr_p.T),
        "w1": np.asarray(L0_gnn_mlp_w1),
        "b1": np.asarray(L0_gnn_mlp_b1).reshape(-1, 1),
        "w2": np.asarray(L0_gnn_mlp_w2),
        "b2": np.asarray(L0_gnn_mlp_b2).reshape(-1, 1),
        "lin_w": np.asarray(L0_gnn_lin_w),
        "lin_b": np.asarray(L0_gnn_lin_b).reshape(1, -1),
    }
    nc = bacc.Bacc("TRN2", target_bir_lowering=False, num_devices=1)
    args = [nc.dram_tensor(n + "_dram", arrays[n].shape, mybir.dt.from_np(arrays[n].dtype), kind="ExternalInput").ap()
            for n in _INS]
    y_dram = nc.dram_tensor("y_dram", (et * P, feats), F32).ap()
    out = nc.dram_tensor("out_dram", (nt * P + QUAD * P, feats), F32, kind="ExternalOutput").ap()
    build(nc, *args, y_dram, out)
    r = run_bass_kernel_spmd(nc, [{n + "_dram": arrays[n] for n in _INS}], core_ids=[0])
    return r.results[0]["out_dram"][:nodes]
```

```python
from contextlib import ExitStack

import concourse.bass as bass
from concourse import mybir

P = 128
F32 = mybir.dt.float32
BF16 = mybir.dt.bfloat16
I32 = mybir.dt.int32
ALU = mybir.AluOpType
ACT = mybir.ActivationFunctionType
AX_X = mybir.AxisListType.X

D = 128
QUAD = 4
BATCH = 16
QUADS = BATCH // QUAD
XSLOTS = 5
EPS = 1e-5
IN_FLIGHT = 3
TOP = 8
POOL_NORM = (1, 1, 1, 1)
RING = 4


def node_tiles(nodes):
    return -(-nodes // (P * BATCH)) * BATCH


def edge_tiles(edges):
    return -(-edges // (P * QUAD)) * QUAD


def build(nc, x, src_cols, src_rows, dst_cols, attr_t, w1, b1, w2, b2, lin_w, lin_b, y_dram, out):
    NT = x.shape[0] // P
    NB = NT // BATCH
    ET = src_cols.shape[1]
    NG = ET // QUAD
    GAUSS = attr_t.shape[0]
    DUMP = x.shape[0]
    WINDOW = IN_FLIGHT - 1
    LAST = NB - 1
    ROUNDS = (NB - 4) // XSLOTS
    assert NB == NG and ROUNDS * XSLOTS == NB - 4 and (NG - 9) % RING == 0

    with ExitStack() as ctx:
        def sb(name, shape, dt=F32):
            return ctx.enter_context(nc.sbuf_tensor(name, shape, dt))

        def sem(name):
            return ctx.enter_context(nc.semaphore(name))

        ident = sb("ident", [P, P])
        ones = sb("ones", [P, P])
        before = sb("before", [P, (WINDOW + 1) * P])
        below = sb("below", [P, P])
        slot_row = sb("slot_row", [P, P])
        slot_row_i = sb("slot_row_i", [P, P], I32)
        dump4_i = sb("dump4_i", [P, QUAD], I32)
        dump4 = sb("dump4", [P, QUAD])
        edge_no_i = sb("edge_no_i", [P, ET], I32)
        edge_no = sb("edge_no", [P, ET])
        zero_rows = sb("zero_rows", [P, QUAD * D])
        w1_sb = sb("w1_sb", [GAUSS, D])
        w2_sb = sb("w2_sb", [P, D])
        lw_sb = sb("lw_sb", [P, D])
        b1_sb = sb("b1_sb", [P, 1])
        b2_sb = sb("b2_sb", [P, 1])
        lb3 = sb("lb3", [3, D])
        lb_res = sb("lb_res", [3, D])
        lb_part = sb("lb_part", [3, 3, D], BF16)
        lb_sel = sb("lb_sel", [3, QUAD, D], BF16)
        ones3 = sb("ones3", [3, P], BF16)
        src_i = sb("src_i", [P, ET], I32)
        src_f = sb("src_f", [P, WINDOW + ET])
        dst_i = sb("dst_i", [P, ET], I32)

        xs = sb("xs", [P, XSLOTS, BATCH, D])
        hn = sb("hn", [P, QUADS, QUAD, D])
        hT = sb("hT", [P, QUADS, QUAD * P])
        stat = sb("stat", [P, XSLOTS, BATCH, 6])
        chain = sb("chain", [P, XSLOTS, 8, BATCH])
        gx = sb("gx", [P, XSLOTS, QUAD, D])
        gidx = sb("gidx", [P, XSLOTS, QUAD], I32)
        xdst = sb("xdst", [P, ET, D])

        attr = xs[0:GAUSS, XSLOTS - 1, :, :].rearrange("p t f -> p (t f)").rearrange("p (s c) -> p s c", s=RING)
        spare = xs[:, 0, :, :].rearrange("p t f -> p (t f)").rearrange("p (s c) -> p s c", s=RING)
        z_sb = spare[:, 0:2, :]
        hTe = spare[:, 2:4, :]
        msg = xs[:, 1, 0:2 * QUAD, :].rearrange("p t f -> p (t f)").rearrange("p (s c) -> p s c", s=2)
        hne = sb("hne", [P, 2, QUAD, D])
        ysb = sb("ysb", [P, RING, QUAD, D])
        srcg = sb("srcg", [P, RING, WINDOW + QUAD])
        clash = sb("clash", [P, RING, QUAD])
        eqs = sb("eqs", [P, QUAD, (WINDOW + 1) * P], BF16)
        flags = sb("flags", [P, ET])
        off = sb("off", [P, RING, QUAD])
        sidx = sb("sidx", [P, RING, QUAD], I32)
        keys = sb("keys", [P, ET])

        top = sb("top", [P, TOP])
        pos = sb("pos", [P, 6, TOP])
        cnt = sb("cnt", [P, 8])
        slow_i = sb("slow_i", [P, 1], I32)
        onehot = sb("onehot", [P, TOP, P])
        lkey = sb("lkey", [P, 4])
        lidx = sb("lidx", [P, 1], I32)
        lsrc_i = sb("lsrc_i", [P, 1], I32)
        rsrc = sb("rsrc", [P, 4])
        same = sb("same", [P, P])
        ridx = sb("ridx", [P, 1], I32)
        ry = sb("ry", [P, D])
        rsum = sb("rsum", [P, D])

        ps = ctx.enter_context(nc.psum_tensor("ps", [P, 8, QUAD * P], F32))

        const_made = sem("const_made")
        ones_set = sem("ones_set")
        loaded = sem("loaded")
        prep = sem("prep")
        lin_b_ready = sem("lin_b_ready")
        x_loaded = [sem(f"x_loaded{s}") for s in range(XSLOTS)]
        out_stored = [sem(f"out_stored{s}") for s in range(XSLOTS)]
        dump_stored = sem("dump_stored")
        chain_step = sem("chain_step")
        var_ready = sem("var_ready")
        sd_ready = sem("sd_ready")
        rstd_ready = sem("rstd_ready")
        stats_ready = sem("stats_ready")
        hn_by_pool = sem("hn_by_pool")
        hn_by_act = sem("hn_by_act")
        turned = [sem(f"turned{q}") for q in range(QUADS)]
        relu_done = [sem(f"relu_done{q}") for q in range(QUADS)]
        lin_done = [sem(f"lin_done{q}") for q in range(QUADS)]
        added = [sem(f"added{q}") for q in range(QUADS)]
        gidx_ready = sem("gidx_ready")
        gathered = [sem(f"gathered{s}") for s in range(XSLOTS)]
        xdst_ready = sem("xdst_ready")

        attr_loaded = [sem(f"attr_loaded{s}") for s in range(RING)]
        e_chain = sem("e_chain")
        e_stats = sem("e_stats")
        e_var = sem("e_var")
        e_sd = sem("e_sd")
        e_rstd = sem("e_rstd")
        e_hn = sem("e_hn")
        e_turned = sem("e_turned")
        e_hT = sem("e_hT")
        z_done = sem("z_done")
        z_relu = sem("z_relu")
        w_done = sem("w_done")
        msg_ready = sem("msg_ready")
        y_done = sem("y_done")
        y_ready = sem("y_ready")
        y_stored = [sem(f"y_stored{s}") for s in range(RING)]
        srcg_ready = sem("srcg_ready")
        rows_ready = sem("rows_ready")
        clash_ready = sem("clash_ready")
        sidx_step = sem("sidx_step")
        sidx_ready = sem("sidx_ready")
        scattered = [sem(f"scattered{k}") for k in range(QUAD)]

        pack_step = sem("pack_step")
        counts_ready = sem("counts_ready")
        base_ready = sem("base_ready")
        onehot_ready = sem("onehot_ready")
        list_ready = sem("list_ready")
        lidx_ready = sem("lidx_ready")
        l_gathered = sem("l_gathered")
        slow_ready = sem("slow_ready")
        r_src = sem("r_src")
        r_row = sem("r_row")
        r_step = sem("r_step")
        r_same = sem("r_same")
        r_sum = sem("r_sum")
        r_ready = sem("r_ready")
        r_scattered = sem("r_scattered")
        r_y = sem("r_y")

        x_by_part = x.rearrange("(p t) f -> p (t f)", t=NT)
        out_by_part = out[0:DUMP, :].rearrange("(p t) f -> p (t f)", t=NT)
        y_by_group = y_dram.rearrange("(g t p) f -> g p t f", t=QUAD, p=P)
        BL = BATCH * D

        def half(g, gm):
            return (g - gm % 2) // 2

        block = ctx.enter_context(nc.Block())

        N_CONST = 6
        N_LOADS = 8
        PREP = 16 * N_LOADS

        @block.sync
        def _(sp):
            sp.dma_start(dst_i[:, :], dst_cols).then_inc(loaded, 16)

            def load(i, s):
                b = i * XSLOTS + s
                sp.dma_start(xs[:, s, :, :].rearrange("p t f -> p (t f)"),
                             x_by_part[:, bass.ts(b, BL)]).then_inc(x_loaded[s], 16)

            def store(i, s):
                b = i * XSLOTS + s
                sp.wait_ge(added[QUADS - 1], b + 1)
                sp.dma_start(out_by_part[:, bass.ts(b, BL)],
                             xs[:, s, :, :].rearrange("p t f -> p (t f)")).then_inc(out_stored[s], 16)

            load(0, 0)
            sp.dma_start(lw_sb[:, :], lin_w).then_inc(loaded, 16)
            sp.dma_start(lb3[:, :], lin_b.to_broadcast([3, D])).then_inc(loaded, 16)
            load(0, 1)
            load(0, 2)
            load(0, 3)
            sp.dma_start(src_i[:, :], src_cols).then_inc(loaded, 16)
            sp.dma_start(w1_sb[:, :], w1).then_inc(loaded, 16)
            sp.dma_start(w2_sb[:, :], w2).then_inc(loaded, 16)
            sp.dma_start(b1_sb[:, :], b1).then_inc(loaded, 16)
            sp.dma_start(b2_sb[:, :], b2).then_inc(loaded, 16)
            sp.wait_ge(ones_set, 1)
            sp.dma_start(out[DUMP:DUMP + QUAD * P, :].rearrange("(p t) f -> p (t f)", t=QUAD),
                         zero_rows[:, :]).then_inc(dump_stored, 16)

            def step(i, s, more):
                if more:
                    before_s = (s + XSLOTS - 1) % XSLOTS
                    if s or not isinstance(i, int) or i:
                        sp.wait_ge(out_stored[before_s], 16 * (i + 1 if s else i))
                    load(i + 1 if s else i, before_s)
                store(i, s)

            step(0, 0, True)
            with sp.Fori(0, ROUNDS - 1) as i:
                for b in range(1, XSLOTS + 1):
                    step(i + b // XSLOTS, b % XSLOTS, True)
            for b in range((ROUNDS - 1) * XSLOTS + 1, NB):
                step(b // XSLOTS, b % XSLOTS, b + XSLOTS - 1 < NB)

            def load_attr(g, s):
                sp.dma_start(attr[:, s, :], attr_t[:, bass.ts(g, QUAD * P)]).then_inc(attr_loaded[s], 16)

            def edge_step(g, gm, more):
                if more:
                    sp.wait_ge(z_done, g + 1)
                    load_attr(g + RING, gm)
                sp.wait_ge(y_ready, g + 1)
                sp.dma_start(y_by_group[g], ysb[:, gm, :, :]).then_inc(y_stored[gm], 16)

            sp.wait_ge(out_stored[XSLOTS - 1], 16 * (NB // XSLOTS))
            for g in range(RING):
                load_attr(g, g)
            with sp.Fori(0, (NG - 5) // RING) as i:
                for gm in range(RING):
                    edge_step(i * RING + gm, gm, True)
            for g in range(NG - 5, NG):
                edge_step(g, g % RING, g + RING < NG)
            for s in range(RING):
                sp.wait_ge(y_stored[s], 16 * ((NG - s + RING - 1) // RING))

            sp.wait_ge(slow_ready, 1)
            slow = sp.value_load(slow_i[0:1, 0:1], min_val=0, max_val=1)
            with sp.If(slow == 1):
                with sp.Fori(0, ET) as t:
                    sp.wait_ge(r_scattered, 16 * (t + 1))
                    sp.dma_start(ry[:, :], y_dram[bass.ts(t, P), :]).then_inc(r_y, 16)

        @block.gpsimd
        def _(pool):
            nc.gpsimd.memset(ident[:, :], 0.0).then_inc(const_made, 1)
            pool.wait_ge(const_made, 1)
            nc.gpsimd.affine_select(out=ident[:, :], in_=ident[:, :], compare_op=ALU.not_equal, fill=1.0,
                                    base=0, pattern=[[-1, P]], channel_multiplier=1).then_inc(const_made, 1)
            nc.gpsimd.iota(slot_row_i[:, :], [[1, P]], base=0, channel_multiplier=0).then_inc(const_made, 1)
            nc.gpsimd.iota(dump4_i[:, :], [[P, QUAD]], base=DUMP, channel_multiplier=1).then_inc(const_made, 1)
            nc.gpsimd.iota(edge_no_i[:, :], [[P, ET]], base=1, channel_multiplier=1).then_inc(const_made, 1)
            pool.wait_ge(ones_set, 2)
            nc.gpsimd.affine_select(out=before[:, WINDOW * P:], in_=before[:, WINDOW * P:],
                                    compare_op=ALU.is_gt, fill=0.0, base=0, pattern=[[-1, P]],
                                    channel_multiplier=1)
            nc.gpsimd.affine_select(out=below[:, :], in_=below[:, :], compare_op=ALU.is_gt, fill=0.0,
                                    base=0, pattern=[[1, P]], channel_multiplier=-1).then_inc(const_made, 1)
            pool.wait_ge(loaded, PREP)

            group_no = pool.alloc_register("group_no")
            landed_before = pool.alloc_register("landed_before")
            landed_now = pool.alloc_register("landed_now")
            round_no = pool.alloc_register("round_no")
            pool.reg_mov(group_no, 0)

            turned_no = pool.alloc_register("turned_no")
            rstd_no = pool.alloc_register("rstd_no")
            pool.reg_mov(rstd_no, 1)

            def norm(s, q, first):
                pool.wait_ge(const_made, 2)
                pool.wait_ge(rstd_ready, rstd_no)
                if not first:
                    pool.wait_ge(turned[q], turned_no)
                for k in range(QUAD - POOL_NORM[q], QUAD):
                    t = q * QUAD + k
                    last = nc.gpsimd.tensor_scalar(hn[:, q, k, :], xs[:, s, t, :], chain[:, s, 6, t:t + 1],
                                                   chain[:, s, 7, t:t + 1], ALU.mult, ALU.add)
                last.then_inc(hn_by_pool, 1)

            def gather(s, k):
                nc.gpsimd.indirect_dma_start(
                    gx[:, s, k, :], None, x,
                    bass.IndirectOffsetOnAxis(ap=gidx[:, s, k:k + 1], axis=0)).then_inc(gathered[s], 16)

            def node_step(b, s, first, more):
                s1 = (s + 1) % XSLOTS
                pool.reg_add(group_no, group_no, 1)
                pool.reg_add(turned_no, rstd_no, -1)
                nc.gpsimd.tensor_copy(gidx[:, s, :], dst_i[:, bass.ts(b, QUAD)]).then_inc(gidx_ready, 1)
                norm(s, 2, first)
                pool.wait_ge(loaded, PREP)
                pool.wait_ge(gidx_ready, group_no)
                gather(s, 0)
                norm(s, 3, first)
                gather(s, 1)
                if more:
                    pool.reg_add(turned_no, turned_no, 1)
                    pool.reg_add(rstd_no, rstd_no, 1)
                    norm(s1, 0, False)
                gather(s, 2)
                if more:
                    norm(s1, 1, False)
                gather(s, 3)

            norm(0, 0, True)
            norm(0, 1, True)
            node_step(0, 0, True, True)
            with pool.Fori(0, ROUNDS) as i:
                for b in range(1, XSLOTS + 1):
                    node_step(i * XSLOTS + b, b % XSLOTS, False, True)
            for b in range(ROUNDS * XSLOTS + 1, NB):
                node_step(b, b % XSLOTS, False, b < LAST)

            for s in range(XSLOTS):
                pool.wait_ge(out_stored[s], 16 * ((NB - s + XSLOTS - 1) // XSLOTS))
            pool.wait_ge(dump_stored, 16)

            def scatter(s, first):
                pool.reg_add(group_no, group_no, 1)
                pool.reg_mov(landed_before, landed_now)
                pool.reg_add(landed_now, landed_now, 16)
                pool.wait_ge(dump_stored, 16)
                pool.wait_ge(y_ready, group_no)
                pool.wait_ge(sidx_ready, group_no)
                for k in range(QUAD):
                    pool.wait_ge(dump_stored, 16)
                    if k < QUAD - 1 and not first:
                        pool.wait_ge(scattered[k + 1], landed_before)
                    elif k == QUAD - 1:
                        pool.wait_ge(scattered[0], landed_now)
                    nc.gpsimd.indirect_dma_start(
                        out, bass.IndirectOffsetOnAxis(ap=sidx[:, s, k:k + 1], axis=0),
                        ysb[:, s, k, :], None, compute_op=ALU.add).then_inc(scattered[k], 16)

            pool.reg_mov(group_no, 0)
            pool.reg_mov(landed_now, 0)
            scatter(0, True)
            with pool.Fori(0, NG // RING) as i:
                for g in range(1, RING + 1):
                    scatter(g % RING, False)
            for k in range(QUAD):
                pool.wait_ge(scattered[k], 16 * NG)

            pool.wait_ge(lidx_ready, 1)
            for s in range(RING):
                pool.wait_ge(y_stored[s], 16 * ((NG - s + RING - 1) // RING))
            nc.gpsimd.indirect_dma_start(
                lsrc_i[:, :], None, src_rows,
                bass.IndirectOffsetOnAxis(ap=lidx[:, :], axis=0)).then_inc(l_gathered, 16)
            nc.gpsimd.indirect_dma_start(
                ry[:, :], None, y_dram,
                bass.IndirectOffsetOnAxis(ap=lidx[:, :], axis=0)).then_inc(l_gathered, 16)

            def add_sums(n):
                pool.reg_add(round_no, round_no, 1)
                pool.wait_ge(dump_stored, 16)
                pool.wait_ge(r_ready, round_no)
                nc.gpsimd.indirect_dma_start(
                    out, bass.IndirectOffsetOnAxis(ap=ridx[:, :], axis=0),
                    rsum[:, :], None, compute_op=ALU.add).then_inc(r_scattered, 16)
                pool.wait_ge(r_scattered, 16 * (n + 1))

            pool.reg_mov(round_no, 0)
            add_sums(0)
            slow = pool.value_load(slow_i[0:1, 0:1], min_val=0, max_val=1)
            with pool.If(slow == 1):
                with pool.Fori(0, ET) as t:
                    add_sums(t + 1)

        @block.tensor
        def _(pe):
            pe.wait_ge(const_made, 2)
            pe.wait_ge(lin_b_ready, 1)
            pe.wait_ge(loaded, PREP)

            def turn(b, q):
                pe.wait_ge(hn_by_act, b * QUADS + q + 1)
                pe.wait_ge(hn_by_pool, b * QUADS + q + 1)
                for k in range(QUAD):
                    last = nc.tensor.transpose(ps[:, q, k * P:(k + 1) * P], hn[:, q, k, :], ident[:, :])
                last.then_inc(turned[q], 1)

            def lin(b, q):
                pe.wait_ge(relu_done[q], b + 1)
                if not isinstance(b, int) or b:
                    pe.wait_ge(added[q], b)
                for k in range(QUAD):
                    nc.tensor.matmul(ps[:, QUADS + q, k * P:(k + 1) * P], hT[:, q, k * P:(k + 1) * P], lw_sb[:, :],
                                     start=(k == 0), stop=False, skip_group_check=True)
                nc.tensor.matmul(ps[:, QUADS + q, :], ones3[:, :], lb_sel[:, :, :].rearrange("p t f -> p (t f)"),
                                 start=False, stop=True, skip_group_check=True).then_inc(lin_done[q], 1)

            def node_step(b, more):
                turn(b, 2)
                lin(b, 0)
                turn(b, 3)
                lin(b, 1)
                if more:
                    turn(b + 1, 0)
                lin(b, 2)
                if more:
                    turn(b + 1, 1)
                lin(b, 3)

            turn(0, 0)
            turn(0, 1)
            node_step(0, True)
            with pe.Fori(0, ROUNDS) as i:
                for b in range(1, XSLOTS + 1):
                    node_step(i * XSLOTS + b, True)
            for b in range(ROUNDS * XSLOTS + 1, NB):
                node_step(b, b < LAST)

            for q in range(QUADS):
                pe.wait_ge(added[q], NB)

            def z(g, gm):
                pe.wait_ge(attr_loaded[gm], 16 * (g // RING + 1) if isinstance(g, int) else 4 * (g - gm) + 16)
                if not isinstance(g, int) or g:
                    pe.wait_ge(z_relu, g)
                nc.tensor.matmul(ps[:, 0, :], w1_sb[:, :], attr[:, gm, :], start=True, stop=True).then_inc(z_done, 1)

            def rows(g, gm):
                pe.wait_ge(srcg_ready, g + 1)
                if not isinstance(g, int) or g >= 2:
                    pe.wait_ge(clash_ready, g - 1)
                for k in range(WINDOW + QUAD):
                    last = nc.tensor.transpose(ps[:, 4 + 2 * (gm % 2) + k // QUAD, (k % QUAD) * P:(k % QUAD + 1) * P],
                                               srcg[:, gm, k:k + 1].to_broadcast([P, P]), ident[:, :])
                last.then_inc(rows_ready, 1)

            def e_lin(g, gm):
                pe.wait_ge(msg_ready, g + 1)
                if not isinstance(g, int) or g:
                    pe.wait_ge(y_ready, g)
                for k in range(QUAD):
                    last = nc.tensor.matmul(ps[:, 3, k * P:(k + 1) * P], msg[:, gm % 2, k * P:(k + 1) * P], lw_sb[:, :],
                                            start=True, stop=True, skip_group_check=True)
                last.then_inc(y_done, 1)

            def edge_step(g, gm, first, more):
                pe.wait_ge(e_hn, g + 1)
                if not first:
                    pe.wait_ge(e_hT, g)
                for k in range(QUAD):
                    last = nc.tensor.transpose(ps[:, 2, k * P:(k + 1) * P], hne[:, gm % 2, k, :], ident[:, :])
                last.then_inc(e_turned, 1)
                if more:
                    z(g + 1, (gm + 1) % RING)
                pe.wait_ge(z_relu, g + 1)
                if not first:
                    pe.wait_ge(msg_ready, g)
                nc.tensor.matmul(ps[:, 1, :], w2_sb[:, :], z_sb[:, gm % 2, :], start=True, stop=True).then_inc(w_done, 1)
                if not first:
                    e_lin(g - 1, (gm + RING - 1) % RING)
                if more:
                    rows(g + 1, (gm + 1) % RING)

            z(0, 0)
            rows(0, 0)
            for g in range(2):
                edge_step(g, g, g == 0, True)
            with pe.Fori(0, (NG - 5) // RING) as i:
                for g in range(2, RING + 2):
                    edge_step(i * RING + g, g % RING, False, True)
            for g in range(NG - 3, NG):
                edge_step(g, g % RING, False, g + 1 < NG)
            e_lin(NG - 1, (NG - 1) % RING)

            pe.wait_ge(counts_ready, 1)
            nc.tensor.matmul(ps[:, 0, 0:1], below[:, :], cnt[:, 0:1], start=True, stop=True)
            nc.tensor.matmul(ps[:, 0, 2:4], ones[:, :], cnt[:, 0:2], start=True, stop=True).then_inc(base_ready, 1)
            pe.wait_ge(onehot_ready, 1)
            for k in range(TOP):
                last = nc.tensor.matmul(ps[:, 1, 0:1], onehot[:, k, :], top[:, k:k + 1],
                                        start=(k == 0), stop=(k == TOP - 1))
            last.then_inc(list_ready, 1)

            def sums(n):
                pe.wait_ge(r_src, n + 1)
                nc.tensor.transpose(ps[:, 2, 0:P], rsrc[:, 0:1].to_broadcast([P, P]), ident[:, :]).then_inc(r_row, 1)
                pe.wait_ge(r_same, n + 1)
                nc.tensor.matmul(ps[:, 3, 0:D], same[:, :], ry[:, :], start=True, stop=True).then_inc(r_sum, 1)

            pe.wait_ge(l_gathered, 32)
            sums(0)
            slow = pe.value_load(slow_i[0:1, 0:1], min_val=0, max_val=1)
            with pe.If(slow == 1):
                with pe.Fori(0, ET) as t:
                    pe.wait_ge(r_y, 16 * (t + 1))
                    sums(t + 1)

        @block.scalar
        def _(act):
            act.wait_ge(loaded, PREP)

            def relu_quad(b, q):
                act.wait_ge(turned[q], b + 1)
                nc.scalar.activation(hT[:, q, :], ps[:, q, :], ACT.Relu).then_inc(relu_done[q], 1)

            def root(b, s):
                act.wait_ge(var_ready, b + 1)
                nc.scalar.activation(chain[:, s, 5, :], chain[:, s, 4, :], ACT.Sqrt).then_inc(sd_ready, 1)

            def norm(b, s, q):
                act.wait_ge(rstd_ready, b + 1)
                for k in range(QUAD - POOL_NORM[q]):
                    t = q * QUAD + k
                    last = nc.scalar.activation(hn[:, q, k, :], xs[:, s, t, :], ACT.Identity,
                                                bias=chain[:, s, 7, t:t + 1], scale=chain[:, s, 6, t:t + 1])
                last.then_inc(hn_by_act, 1)

            def put(g, i, s):
                act.wait_ge(gathered[s], 16 * QUAD * (i + 1))
                nc.scalar.activation(xdst[:, bass.ts(g, QUAD), :].rearrange("p t f -> p (t f)"),
                                     gx[:, s, :, :].rearrange("p t f -> p (t f)"), ACT.Copy).then_inc(xdst_ready, 1)

            root(0, 0)
            norm(0, 0, 0)
            norm(0, 0, 1)

            def node_step(i, s, first, more):
                b = i * XSLOTS + s
                s1 = (s + 1) % XSLOTS
                norm(b, s, 2)
                if more:
                    root(b + 1, s1)
                relu_quad(b, 0)
                norm(b, s, 3)
                relu_quad(b, 1)
                if more:
                    norm(b + 1, s1, 0)
                relu_quad(b, 2)
                if more:
                    norm(b + 1, s1, 1)
                if not first:
                    put(b - 1, i if s else i - 1, (s + XSLOTS - 1) % XSLOTS)
                relu_quad(b, 3)

            node_step(0, 0, True, True)
            with act.Fori(0, ROUNDS) as i:
                for b in range(1, XSLOTS + 1):
                    node_step(i + b // XSLOTS, b % XSLOTS, False, True)
            for b in range(ROUNDS * XSLOTS + 1, NB):
                node_step(b // XSLOTS, b % XSLOTS, False, b < LAST)
            put(LAST, LAST // XSLOTS, LAST % XSLOTS)

            act.wait_ge(out_stored[0], 16 * (NB // XSLOTS + 1))

            def relu_z(g, s):
                act.wait_ge(z_done, g + 1)
                nc.scalar.activation(z_sb[:, s, :], ps[:, 0, :], ACT.Relu, bias=b1_sb[:, 0:1]).then_inc(z_relu, 1)

            def e_root(pair, h, n):
                act.wait_ge(e_var, pair + 1)
                nc.scalar.activation(chain[:, h, 5, 0:n], chain[:, h, 4, 0:n], ACT.Sqrt).then_inc(e_sd, 1)

            def e_norm(g, gm):
                act.wait_ge(e_rstd, g // 2 + 1 if isinstance(g, int) else half(g, gm) + 1)
                for k in range(QUAD):
                    c = (gm % 2) * QUAD + k
                    last = nc.scalar.activation(hne[:, gm % 2, k, :],
                                                xdst[:, bass.ds(g * QUAD + k, 1), :].rearrange("p t f -> p (t f)"),
                                                ACT.Identity, bias=chain[:, gm // 2, 7, c:c + 1],
                                                scale=chain[:, gm // 2, 6, c:c + 1])
                last.then_inc(e_hn, 1)

            def y_rows(g, gm, reused):
                act.wait_ge(y_done, g + 1)
                if reused:
                    for k in range(QUAD):
                        act.wait_ge(scattered[k], 16 * (g - 3))
                    act.wait_ge(y_stored[gm], 4 * (g - gm))
                nc.scalar.activation(ysb[:, gm, :, :].rearrange("p t f -> p (t f)"), ps[:, 3, :],
                                     ACT.Copy).then_inc(y_ready, 1)

            def edge_step(g, gm, pair, more, root_n, reused):
                act.wait_ge(e_turned, g + 1)
                nc.scalar.activation(hTe[:, gm % 2, :], ps[:, 2, :], ACT.Relu).then_inc(e_hT, 1)
                if more:
                    relu_z(g + 1, (gm + 1) % 2)
                    e_norm(g + 1, (gm + 1) % RING)
                if root_n:
                    e_root(pair + 1, ((gm + 2) % RING) // 2, root_n)
                if not isinstance(g, int) or g:
                    y_rows(g - 1, (gm + RING - 1) % RING, reused)

            def peeled(g):
                root_n = 0 if g % 2 or g + 2 >= NG else QUAD * min(2, NG - g - 2)
                edge_step(g, g % RING, g // 2, g + 1 < NG, root_n, g >= 5)

            relu_z(0, 0)
            e_root(0, 0, 2 * QUAD)
            e_norm(0, 0)
            for g in range(6):
                peeled(g)
            with act.Fori(1, (NG - 5) // RING) as i:
                for g in range(2, RING + 2):
                    edge_step(i * RING + g, g % RING, i * 2 + g // 2, True, 0 if g % 2 else 2 * QUAD, True)
            for g in range(NG - 3, NG):
                peeled(g)
            y_rows(NG - 1, (NG - 1) % RING, True)

        @block.vector
        def _(dve):
            nc.vector.memset(zero_rows[:, :], 0.0).then_inc(ones_set, 1)
            nc.vector.memset(ones[:, :], 1.0)
            nc.vector.memset(below[:, :], 1.0)
            nc.vector.memset(before[:, :], 1.0).then_inc(ones_set, 1)
            nc.vector.memset(ones3[:, :], 1.0)
            nc.vector.memset(src_f[:, 0:WINDOW], -1.0)
            done = [0]

            def then(ins):
                done[0] += 1
                ins.then_inc(prep, 1)
                dve.wait_ge(prep, done[0])

            dve.wait_ge(loaded, PREP)
            dve.wait_ge(const_made, 5)
            nc.vector.tensor_copy(src_f[:, WINDOW:], src_i[:, :])
            nc.vector.tensor_copy(slot_row[:, :], slot_row_i[:, :])
            nc.vector.tensor_copy(dump4[:, :], dump4_i[:, :])
            nc.vector.tensor_copy(edge_no[:, :], edge_no_i[:, :])
            then(nc.vector.tensor_copy(lb_part[:, 0, :], lb3[:, :]))
            then(nc.vector.tensor_tensor(lb_res[:, :], lb3[:, :], lb_part[:, 0, :], ALU.subtract))
            then(nc.vector.tensor_copy(lb_part[:, 1, :], lb_res[:, :]))
            then(nc.vector.tensor_tensor(lb_res[:, :], lb_res[:, :], lb_part[:, 1, :], ALU.subtract))
            then(nc.vector.tensor_copy(lb_part[:, 2, :], lb_res[:, :]))
            then(nc.vector.tensor_scalar(lb_sel[:, 0, :], lb_part[:, 0, :], ident[0:3, 0:1], None, ALU.mult))
            for k in (1, 2):
                then(nc.vector.scalar_tensor_tensor(out=lb_sel[:, 0, :], in0=lb_part[:, k, :], scalar=ident[0:3, k:k + 1],
                                                    in1=lb_sel[:, 0, :], op0=ALU.mult, op1=ALU.add))
            for k in range(1, QUAD):
                then(nc.vector.tensor_copy(lb_sel[:, k, :], lb_sel[:, 0, :]))
            dve.sem_inc(lin_b_ready, 1)

            def chain_steps(n, h, b, done, var_sem, sd_sem, rstd_sem):
                STEPS = 9

                def after(k):
                    dve.wait_ge(done, b * STEPS + k)
                st = stat[:, h, 0:n, :]
                c = lambda r: chain[:, h, r, 0:n]

                def halves():
                    nc.vector.tensor_tensor(c(1), st[:, :, 1], st[:, :, 4], ALU.subtract).then_inc(done, 1)
                    nc.vector.tensor_tensor(c(2), st[:, :, 2], st[:, :, 5], ALU.add).then_inc(done, 1)
                    nc.vector.tensor_tensor(c(0), st[:, :, 1], st[:, :, 4], ALU.add).then_inc(done, 1)

                def between():
                    after(1)
                    nc.vector.scalar_tensor_tensor(out=c(3), in0=c(1), scalar=float(D // 4), in1=c(1),
                                                   op0=ALU.mult, op1=ALU.mult).then_inc(done, 1)

                def total():
                    after(4)
                    nc.vector.tensor_tensor(c(1), c(2), c(3), ALU.add).then_inc(done, 1)

                def variance():
                    after(5)
                    nc.vector.tensor_scalar(c(4), c(1), 1.0 / D, EPS, ALU.mult, ALU.add).then_inc(var_sem, 1)

                def inverse():
                    dve.wait_ge(sd_sem, b + 1)
                    nc.vector.reciprocal(c(1), c(5)).then_inc(done, 1)

                def newton1():
                    after(6)
                    nc.vector.tensor_tensor(c(2), c(1), c(1), ALU.mult).then_inc(done, 1)

                def newton2():
                    after(7)
                    nc.vector.scalar_tensor_tensor(out=c(3), in0=c(2), scalar=-0.5, in1=c(4),
                                                   op0=ALU.mult, op1=ALU.mult).then_inc(done, 1)

                def newton3():
                    after(8)
                    nc.vector.scalar_tensor_tensor(out=c(6), in0=c(3), scalar=1.5, in1=c(1),
                                                   op0=ALU.add, op1=ALU.mult).then_inc(done, 1)

                def shift():
                    after(9)
                    nc.vector.scalar_tensor_tensor(out=c(7), in0=c(0), scalar=-0.5, in1=c(6),
                                                   op0=ALU.mult, op1=ALU.mult).then_inc(rstd_sem, 1)

                return halves, between, total, variance, inverse, newton1, newton2, newton3, shift

            def add_quad(b, s, q):
                dve.wait_ge(lin_done[q], b + 1)
                x_quad = xs[:, s, q * QUAD:(q + 1) * QUAD, :].rearrange("p t f -> p (t f)")
                nc.vector.tensor_tensor(x_quad, ps[:, QUADS + q, :], x_quad, ALU.add).then_inc(added[q], 1)

            def bn(s, *tiles):
                for t in tiles:
                    ins = nc.vector.bn_stats(stat[:, s, t, :], xs[:, s, t, :])
                    if t == BATCH - 1:
                        ins.then_inc(stats_ready, 1)

            def node_step(i, s, first, bn_more, chain_more):
                b = i * XSLOTS + s
                s1, s2 = (s + 1) % XSLOTS, (s + 2) % XSLOTS

                def stats(*tiles):
                    if bn_more:
                        bn(s2, *tiles)

                if chain_more:
                    steps = chain_steps(BATCH, s1, b + 1, chain_step, var_ready, sd_ready, rstd_ready)
                else:
                    steps = [lambda: None] * 9
                if bn_more:
                    dve.wait_ge(x_loaded[s2], 16 * (i + 1 + (s + 2) // XSLOTS))
                    next_steps = chain_steps(BATCH, s2, b + 2, chain_step, var_ready, sd_ready, rstd_ready)
                else:
                    next_steps = [lambda: None] * 9
                stats(0, 1)
                if not first:
                    add_quad(b - 1, (s + XSLOTS - 1) % XSLOTS, 3)
                steps[4]()
                stats(2)
                steps[5]()
                stats(3)
                steps[6]()
                stats(4)
                steps[7]()
                stats(5)
                steps[8]()
                stats(6, 7)
                add_quad(b, s, 0)
                stats(8, 9, 10, 11, 12)
                add_quad(b, s, 1)
                stats(13, 14, 15)
                if bn_more:
                    dve.wait_ge(stats_ready, b + 3)
                next_steps[0]()
                next_steps[1]()
                add_quad(b, s, 2)
                next_steps[2]()
                next_steps[3]()

            dve.wait_ge(x_loaded[0], 16)
            bn(0, *range(BATCH))
            dve.wait_ge(x_loaded[1], 16)
            bn(1, *range(BATCH))
            dve.wait_ge(stats_ready, 1)
            for step in chain_steps(BATCH, 0, 0, chain_step, var_ready, sd_ready, rstd_ready):
                step()
            dve.wait_ge(stats_ready, 2)
            for step in chain_steps(BATCH, 1, 1, chain_step, var_ready, sd_ready, rstd_ready)[:4]:
                step()
            node_step(0, 0, True, True, True)
            with dve.Fori(0, ROUNDS) as i:
                for b in range(1, XSLOTS + 1):
                    node_step(i + b // XSLOTS, b % XSLOTS, False, True, True)
            for b in range(ROUNDS * XSLOTS + 1, NB):
                node_step(b // XSLOTS, b % XSLOTS, False, b + 2 < NB, b + 1 < NB)
            add_quad(LAST, LAST % XSLOTS, 3)

            dve.wait_ge(out_stored[1], 16 * (NB // XSLOTS + 1))

            def e_bn(g, gm):
                dve.wait_ge(xdst_ready, g + 1)
                for k in range(QUAD):
                    last = nc.vector.bn_stats(stat[:, gm // 2, (gm % 2) * QUAD + k, :],
                                              xdst[:, bass.ds(g * QUAD + k, 1), :].rearrange("p t f -> p (t f)"))
                last.then_inc(e_stats, 1)

            def sources(g, gm):
                if not isinstance(g, int) or g >= RING:
                    dve.wait_ge(sidx_ready, g - 3)
                nc.vector.tensor_copy(srcg[:, gm, :], src_f[:, bass.ds(g * QUAD, WINDOW + QUAD)]).then_inc(srcg_ready, 1)

            def clashes(g, gm, k):
                both = ps[:, 4 + 2 * (gm % 2):6 + 2 * (gm % 2), :].rearrange("p b c -> p (b c)")
                last = nc.vector.scalar_tensor_tensor(
                    out=eqs[:, k, :], in0=both[:, k * P:(k + WINDOW + 1) * P], scalar=srcg[:, gm, WINDOW + k:WINDOW + k + 1],
                    in1=before[:, :], op0=ALU.is_equal, op1=ALU.mult, accum_out=clash[:, gm, k:k + 1])
                if k == QUAD - 1:
                    last.then_inc(clash_ready, 1)

            def targets(g, gm, reused):
                own = srcg[:, gm, WINDOW:]

                def away():
                    nc.vector.tensor_tensor(off[:, gm, :], dump4[:, :], own, ALU.subtract).then_inc(sidx_step, 1)

                def put_off():
                    dve.wait_ge(clash_ready, g + 1)
                    nc.vector.scalar_tensor_tensor(out=keys[:, bass.ds(g * QUAD, QUAD)], in0=clash[:, gm, :], scalar=1.0,
                                                   in1=edge_no[:, bass.ds(g * QUAD, QUAD)],
                                                   op0=ALU.min, op1=ALU.mult).then_inc(sidx_step, 1)
                    dve.wait_ge(sidx_step, g * 3 + 1)
                    nc.vector.scalar_tensor_tensor(out=off[:, gm, :], in0=clash[:, gm, :], scalar=1.0, in1=off[:, gm, :],
                                                   op0=ALU.min, op1=ALU.mult).then_inc(sidx_step, 1)

                def target():
                    if reused:
                        for k in range(QUAD):
                            dve.wait_ge(scattered[k], 16 * (g - 3))
                    dve.wait_ge(sidx_step, g * 3 + 3)
                    nc.vector.tensor_tensor(sidx[:, gm, :], off[:, gm, :], own, ALU.add).then_inc(sidx_ready, 1)

                return away, put_off, target

            def message(g, s):
                dve.wait_ge(w_done, g + 1)
                dve.wait_ge(e_hT, g + 1)
                if not isinstance(g, int) or g >= 2:
                    dve.wait_ge(y_done, g - 1)
                nc.vector.scalar_tensor_tensor(out=msg[:, s, :], in0=ps[:, 1, :], scalar=b2_sb[:, 0:1], in1=hTe[:, s, :],
                                               op0=ALU.add, op1=ALU.mult).then_inc(msg_ready, 1)

            def edge_step(g, gm, pair, chain_n, bn_more, src_more, reused):
                if chain_n:
                    steps = chain_steps(chain_n, ((gm + 2) % RING) // 2, pair + 1, e_chain, e_var, e_sd, e_rstd)
                else:
                    steps = [lambda: None] * 9
                away, put_off, target = targets(g, gm, reused)
                if bn_more:
                    e_bn(g + 3, (gm + 3) % RING)
                away()
                if src_more:
                    sources(g + 2, (gm + 2) % RING)
                if chain_n:
                    dve.wait_ge(e_stats, g + (4 if chain_n == 2 * QUAD else 3))
                dve.wait_ge(rows_ready, g + 1)
                steps[0]()
                clashes(g, gm, 0)
                steps[1]()
                clashes(g, gm, 1)
                steps[2]()
                clashes(g, gm, 2)
                steps[3]()
                clashes(g, gm, 3)
                message(g, gm % 2)
                steps[4]()
                put_off()
                steps[5]()
                target()
                steps[6]()
                steps[7]()
                steps[8]()

            def peeled(g):
                chain_n = 0 if g % 2 or g + 2 >= NG else QUAD * min(2, NG - g - 2)
                edge_step(g, g % RING, g // 2, chain_n, g + 3 < NG, g + 2 < NG, g >= RING)

            for g in range(3):
                e_bn(g, g)
            sources(0, 0)
            sources(1, 1)
            dve.wait_ge(e_stats, 2)
            for step in chain_steps(2 * QUAD, 0, 0, e_chain, e_var, e_sd, e_rstd):
                step()
            for g in range(6):
                peeled(g)
            with dve.Fori(1, (NG - 5) // RING) as i:
                for g in range(2, RING + 2):
                    edge_step(i * RING + g, g % RING, i * 2 + g // 2, 0 if g % 2 else 2 * QUAD, True, True, True)
            for g in range(NG - 3, NG):
                peeled(g)

            packed = [0]

            def link(ins):
                packed[0] += 1
                ins.then_inc(pack_step, 1)
                dve.wait_ge(pack_step, packed[0])

            dve.wait_ge(sidx_step, 3 * NG)
            link(nc.vector.max(top[:, :], keys[:, :]))
            link(nc.vector.tensor_scalar(pos[:, 0, :], top[:, :], 0.0, None, ALU.is_gt))
            link(nc.vector.tensor_reduce(cnt[:, 0:1], pos[:, 0, :], AX_X, ALU.add))
            link(nc.vector.tensor_scalar(flags[:, :], keys[:, :], 0.0, None, ALU.is_gt))
            nc.vector.tensor_reduce(cnt[:, 1:2], flags[:, :], AX_X, ALU.add).then_inc(counts_ready, 1)
            dve.wait_ge(base_ready, 1)
            link(nc.vector.tensor_copy(cnt[:, 2:3], ps[:, 0, 0:1]))
            link(nc.vector.tensor_copy(cnt[:, 3:5], ps[:, 0, 2:4]))
            link(nc.vector.tensor_tensor(cnt[:, 5:6], cnt[:, 4:5], cnt[:, 3:4], ALU.is_gt))
            link(nc.vector.tensor_scalar(cnt[:, 6:7], cnt[:, 4:5], float(P), None, ALU.is_gt))
            link(nc.vector.tensor_tensor(cnt[:, 5:6], cnt[:, 5:6], cnt[:, 6:7], ALU.max))
            link(nc.vector.tensor_copy(slow_i[:, :], cnt[:, 5:6]))
            link(nc.vector.tensor_scalar(cnt[:, 6:7], cnt[:, 5:6], -1.0, 1.0, ALU.mult, ALU.add))
            link(nc.vector.tensor_scalar(pos[:, 1, :], pos[:, 0, :], cnt[:, 6:7], None, ALU.mult))
            link(nc.vector.tensor_scalar(pos[:, 2, :], slot_row[:, 0:TOP], cnt[:, 2:3], 1.0, ALU.add, ALU.add))
            link(nc.vector.tensor_tensor(pos[:, 3, :], pos[:, 2, :], pos[:, 1, :], ALU.mult))
            link(nc.vector.tensor_scalar(pos[:, 4, :], pos[:, 3, :], 1.0, None, ALU.subtract))
            for k in range(TOP):
                last = nc.vector.tensor_scalar(onehot[:, k, :], slot_row[:, :], pos[:, 4, k:k + 1], None, ALU.is_equal)
            last.then_inc(onehot_ready, 1)
            dve.wait_ge(list_ready, 1)
            link(nc.vector.tensor_copy(lkey[:, 0:1], ps[:, 1, 0:1]))
            link(nc.vector.tensor_scalar(lkey[:, 1:2], lkey[:, 0:1], 1.0, None, ALU.min))
            link(nc.vector.tensor_tensor(lkey[:, 2:3], lkey[:, 0:1], lkey[:, 1:2], ALU.subtract))
            nc.vector.tensor_copy(lidx[:, :], lkey[:, 2:3]).then_inc(lidx_ready, 1)
            dve.wait_ge(l_gathered, 32)
            dump = dump4[:, QUAD - 1:QUAD]

            def pick(source, taken, n, wait):
                wait(nc.vector.tensor_tensor(rsrc[:, 1:2], source, dump, ALU.subtract))
                wait(nc.vector.tensor_tensor(rsrc[:, 2:3], rsrc[:, 1:2], taken, ALU.mult))
                nc.vector.tensor_tensor(rsrc[:, 0:1], rsrc[:, 2:3], dump, ALU.add).then_inc(r_src, 1)

            def sums(n, wait):
                dve.wait_ge(r_src, n + 1)
                dve.wait_ge(r_row, n + 1)
                nc.vector.tensor_scalar(same[:, :], ps[:, 2, 0:P], rsrc[:, 0:1], None, ALU.is_equal).then_inc(r_same, 1)
                wait(nc.vector.scalar_tensor_tensor(out=eqs[:, 0, 0:P], in0=ps[:, 2, 0:P], scalar=rsrc[:, 0:1],
                                                    in1=before[:, WINDOW * P:], op0=ALU.is_equal, op1=ALU.mult,
                                                    accum_out=lkey[:, 3:4]))
                wait(nc.vector.tensor_tensor(rsrc[:, 1:2], dump, rsrc[:, 0:1], ALU.subtract))
                wait(nc.vector.scalar_tensor_tensor(out=rsrc[:, 2:3], in0=lkey[:, 3:4], scalar=1.0, in1=rsrc[:, 1:2],
                                                    op0=ALU.min, op1=ALU.mult))
                wait(nc.vector.tensor_tensor(ridx[:, :], rsrc[:, 2:3], rsrc[:, 0:1], ALU.add))
                dve.wait_ge(r_sum, n + 1)
                nc.vector.tensor_copy(rsum[:, :], ps[:, 3, 0:D]).then_inc(r_ready, 1)

            link(nc.vector.tensor_copy(rsrc[:, 3:4], lsrc_i[:, :]))
            pick(rsrc[:, 3:4], lkey[:, 1:2], 0, link)
            sums(0, link)
            dve.sem_inc(slow_ready, 1)

            slow = dve.value_load(slow_i[0:1, 0:1], min_val=0, max_val=1)
            with dve.If(slow == 1):
                with dve.Fori(0, ET) as t:
                    n = t + 1
                    k = [0]

                    def turn(ins):
                        k[0] += 1
                        ins.then_inc(r_step, 1)
                        dve.wait_ge(r_step, t * 8 + k[0])

                    dve.wait_ge(r_scattered, 16 * n)
                    turn(nc.vector.tensor_scalar(lkey[:, 1:2], keys[:, bass.ds(t, 1)], 1.0, None, ALU.min))
                    turn(nc.vector.tensor_copy(rsrc[:, 3:4], src_f[:, bass.ds(t + WINDOW, 1)]))
                    pick(rsrc[:, 3:4], lkey[:, 1:2], n, turn)
                    sums(n, turn)


_INS = ["x", "src_cols", "src_rows", "dst_cols", "attr_t", "w1", "b1", "w2", "b2", "lin_w", "lin_b"]


def kernel(x, src, dst, edge_attr_50, edge_weight, L0_gnn_mlp_w1, L0_gnn_mlp_b1, L0_gnn_mlp_w2, L0_gnn_mlp_b2,
           L0_gnn_lin_w, L0_gnn_lin_b):
    import numpy as np
    import concourse.bacc as bacc
    from concourse.bass_utils import run_bass_kernel_spmd

    nodes, feats = x.shape
    edges = src.shape[0]
    nt, et = node_tiles(nodes), edge_tiles(edges)

    def padded(a, rows, fill):
        full = np.empty((rows,) + a.shape[1:], a.dtype)
        full[:a.shape[0]] = a
        full[a.shape[0]:] = fill
        return full

    pads = np.arange(edges, et * P)
    dump_rows = (nt * P + (pads // P % QUAD) * P + pads % P).astype(np.int32)
    src_p = padded(np.asarray(src), et * P, dump_rows)
    dst_p = padded(np.asarray(dst), et * P, 0)
    attr_p = padded(np.asarray(edge_attr_50), et * P, 0)
    arrays = {
        "x": padded(np.asarray(x), nt * P, 0),
        "src_cols": np.ascontiguousarray(src_p.reshape(et, P).T),
        "src_rows": src_p.reshape(et * P, 1),
        "dst_cols": np.ascontiguousarray(dst_p.reshape(et, P).T),
        "attr_t": np.ascontiguousarray(attr_p.T),
        "w1": np.asarray(L0_gnn_mlp_w1),
        "b1": np.asarray(L0_gnn_mlp_b1).reshape(-1, 1),
        "w2": np.asarray(L0_gnn_mlp_w2),
        "b2": np.asarray(L0_gnn_mlp_b2).reshape(-1, 1),
        "lin_w": np.asarray(L0_gnn_lin_w),
        "lin_b": np.asarray(L0_gnn_lin_b).reshape(1, -1),
    }
    nc = bacc.Bacc("TRN2", target_bir_lowering=False, num_devices=1)
    args = [nc.dram_tensor(n + "_dram", arrays[n].shape, mybir.dt.from_np(arrays[n].dtype), kind="ExternalInput").ap()
            for n in _INS]
    y_dram = nc.dram_tensor("y_dram", (et * P, feats), F32).ap()
    out = nc.dram_tensor("out_dram", (nt * P + QUAD * P, feats), F32, kind="ExternalOutput").ap()
    build(nc, *args, y_dram, out)
    r = run_bass_kernel_spmd(nc, [{n + "_dram": arrays[n] for n in _INS}], core_ids=[0])
    return r.results[0]["out_dram"][:nodes]
```

```python
from contextlib import ExitStack

import concourse.bass as bass
from concourse import mybir

P = 128
F32 = mybir.dt.float32
BF16 = mybir.dt.bfloat16
I32 = mybir.dt.int32
ALU = mybir.AluOpType
ACT = mybir.ActivationFunctionType
AX_X = mybir.AxisListType.X

D = 128
QUAD = 4
BATCH = 16
QUADS = BATCH // QUAD
XSLOTS = 6
AHEAD = 4
GSLOTS = 3
EPS = 1e-5
IN_FLIGHT = 3
TOP = 8
POOL_NORM = (1, 1, 1, 2)
RING = 4


def node_tiles(nodes):
    return -(-nodes // (P * BATCH)) * BATCH


def edge_tiles(edges):
    return -(-edges // (P * QUAD)) * QUAD


def build(nc, x, src_cols, src_rows, dst_cols, attr_t, w1, b1, w2, b2, lin_w, lin_b, y_dram, out):
    NT = x.shape[0] // P
    NB = NT // BATCH
    ET = src_cols.shape[1]
    NG = ET // QUAD
    GAUSS = attr_t.shape[0]
    DUMP = x.shape[0]
    WINDOW = IN_FLIGHT - 1
    LAST = NB - 1
    ROUNDS = (NB - 4) // XSLOTS
    assert NB == NG and XSLOTS % GSLOTS == 0 and XSLOTS % 2 == 0 and (NG - 9) % RING == 0

    with ExitStack() as ctx:
        def sb(name, shape, dt=F32):
            return ctx.enter_context(nc.sbuf_tensor(name, shape, dt))

        def sem(name):
            return ctx.enter_context(nc.semaphore(name))

        ident = sb("ident", [P, P])
        ones = sb("ones", [P, P])
        before = sb("before", [P, (WINDOW + 1) * P])
        below = sb("below", [P, P])
        slot_row = sb("slot_row", [P, P])
        slot_row_i = sb("slot_row_i", [P, P], I32)
        dump4_i = sb("dump4_i", [P, QUAD], I32)
        dump4 = sb("dump4", [P, QUAD])
        edge_no_i = sb("edge_no_i", [P, ET], I32)
        edge_no = sb("edge_no", [P, ET])
        warm = sb("warm", [P, 1])
        zero_rows = sb("zero_rows", [P, QUAD * D])
        w1_sb = sb("w1_sb", [GAUSS, D])
        w2_sb = sb("w2_sb", [P, D])
        lw_sb = sb("lw_sb", [P, D])
        b1_sb = sb("b1_sb", [P, 1])
        b2_sb = sb("b2_sb", [P, 1])
        lb3 = sb("lb3", [3, D])
        lb_res = sb("lb_res", [3, D])
        lb_part = sb("lb_part", [3, 3, D], BF16)
        lb_sel = sb("lb_sel", [3, QUAD, D], BF16)
        ones3 = sb("ones3", [3, P], BF16)
        src_i = sb("src_i", [P, ET], I32)
        src_f = sb("src_f", [P, WINDOW + ET])
        dst_i = sb("dst_i", [P, ET], I32)

        xs = sb("xs", [P, XSLOTS, BATCH, D])
        hn = sb("hn", [P, QUADS, QUAD, D])
        hT = sb("hT", [P, QUADS, QUAD * P])
        stat = sb("stat", [P, XSLOTS, BATCH, 6])
        chain = sb("chain", [P, XSLOTS, 8, BATCH])
        gx = sb("gx", [P, GSLOTS, QUAD, D])
        gidx = sb("gidx", [P, XSLOTS, QUAD], I32)
        xdst = sb("xdst", [P, ET, D])

        attr = xs[0:GAUSS, 1, :, :].rearrange("p t f -> p (t f)").rearrange("p (s c) -> p s c", s=RING)
        spare = xs[:, 2, :, :].rearrange("p t f -> p (t f)").rearrange("p (s c) -> p s c", s=RING)
        z_sb = spare[:, 0:2, :]
        hTe = spare[:, 2:4, :]
        msg = xs[:, 3, 0:2 * QUAD, :].rearrange("p t f -> p (t f)").rearrange("p (s c) -> p s c", s=2)
        hne = sb("hne", [P, 2, QUAD, D])
        ysb = sb("ysb", [P, RING, QUAD, D])
        srcg = sb("srcg", [P, RING, WINDOW + QUAD])
        clash = sb("clash", [P, RING, QUAD])
        eqs = sb("eqs", [P, QUAD, (WINDOW + 1) * P], BF16)
        flags = sb("flags", [P, ET])
        off = sb("off", [P, ET])
        sidx = sb("sidx", [P, RING, QUAD], I32)
        keys = sb("keys", [P, ET])

        top = sb("top", [P, TOP])
        pos = sb("pos", [P, 4, TOP])
        cnt = sb("cnt", [P, 8])
        slow_i = sb("slow_i", [P, 1], I32)
        onehot = xs[:, 4, 0:TOP, :]
        lkey = sb("lkey", [P, 4])
        lidx = sb("lidx", [P, 1], I32)
        lsrc_i = sb("lsrc_i", [P, 1], I32)
        rsrc = sb("rsrc", [P, 4])
        same = sb("same", [P, P])
        ridx = sb("ridx", [P, 1], I32)
        ry = sb("ry", [P, D])
        rsum = sb("rsum", [P, D])

        ps = ctx.enter_context(nc.psum_tensor("ps", [P, 8, QUAD * P], F32))

        const_made = sem("const_made")
        ones_set = sem("ones_set")
        lin_b_loaded = sem("lin_b_loaded")
        loaded = sem("loaded")
        e_loaded = sem("e_loaded")
        prep = sem("prep")
        src_ready = sem("src_ready")
        lin_b_ready = sem("lin_b_ready")
        x_loaded = [sem(f"x_loaded{s}") for s in range(XSLOTS)]
        out_stored = [sem(f"out_stored{s}") for s in range(XSLOTS)]
        first_loaded = [sem(f"first_loaded{h}") for h in range(2)]
        dump_stored = sem("dump_stored")
        chain_step = sem("chain_step")
        var_ready = sem("var_ready")
        sd_ready = sem("sd_ready")
        rstd_ready = sem("rstd_ready")
        stats_ready = sem("stats_ready")
        hn_by_pool = sem("hn_by_pool")
        hn_by_act = sem("hn_by_act")
        turned = [sem(f"turned{q}") for q in range(QUADS)]
        relu_done = [sem(f"relu_done{q}") for q in range(QUADS)]
        lin_done = [sem(f"lin_done{q}") for q in range(QUADS)]
        added = [sem(f"added{q}") for q in range(QUADS)]
        gidx_ready = sem("gidx_ready")
        gathered = [sem(f"gathered{s}") for s in range(GSLOTS)]
        xdst_by_act = sem("xdst_by_act")
        xdst_by_dve = sem("xdst_by_dve")

        attr_loaded = [sem(f"attr_loaded{s}") for s in range(RING)]
        e_chain = sem("e_chain")
        e_stats = sem("e_stats")
        e_var = sem("e_var")
        e_sd = sem("e_sd")
        e_rstd = sem("e_rstd")
        e_hn = sem("e_hn")
        e_turned = sem("e_turned")
        e_hT = sem("e_hT")
        z_done = sem("z_done")
        z_relu = sem("z_relu")
        w_done = sem("w_done")
        msg_ready = sem("msg_ready")
        y_done = sem("y_done")
        y_ready = sem("y_ready")
        y_stored = [sem(f"y_stored{s}") for s in range(RING)]
        srcg_ready = sem("srcg_ready")
        rows_ready = sem("rows_ready")
        clash_ready = sem("clash_ready")
        off_ready = sem("off_ready")
        sidx_ready = sem("sidx_ready")
        landed = sem("landed")
        scattered = [sem(f"scattered{k}") for k in range(QUAD)]

        pack_step = sem("pack_step")
        counts_ready = sem("counts_ready")
        base_ready = sem("base_ready")
        onehot_ready = sem("onehot_ready")
        list_ready = sem("list_ready")
        lidx_ready = sem("lidx_ready")
        lsrc_gathered = sem("lsrc_gathered")
        ry_gathered = sem("ry_gathered")
        slow_ready = sem("slow_ready")
        r_src = sem("r_src")
        r_row = sem("r_row")
        r_step = sem("r_step")
        r_same = sem("r_same")
        r_sum = sem("r_sum")
        r_ready = sem("r_ready")
        r_scattered = sem("r_scattered")
        r_y = sem("r_y")

        x_by_part = x.rearrange("(p t) f -> p (t f)", t=NT)
        out_by_part = out[0:DUMP, :].rearrange("(p t) f -> p (t f)", t=NT)
        y_by_group = y_dram.rearrange("(g t p) f -> g p t f", t=QUAD, p=P)
        BL = BATCH * D

        def half(g, gm):
            return (g - gm % 2) // 2

        block = ctx.enter_context(nc.Block())

        N_CONST = 6
        PREP = 16 * 2
        E_PREP = 16 * 5

        def uses(s):
            return (NB - s + XSLOTS - 1) // XSLOTS

        STORES = [16 * uses(s) for s in range(XSLOTS)]
        STORES[LAST % XSLOTS] += 16 * (QUADS - 1)
        LOOP = 2 * RING
        PAIR0 = 2

        @block.sync
        def _(sp):
            def load(i, s):
                b = i * XSLOTS + s
                sp.dma_start(xs[:, s, :, :].rearrange("p t f -> p (t f)"),
                             x_by_part[:, bass.ts(b, BL)]).then_inc(x_loaded[s], 16)

            def store(i, s):
                b = i * XSLOTS + s
                sp.wait_ge(added[QUADS - 1], b + 1)
                sp.dma_start(out_by_part[:, bass.ts(b, BL)],
                             xs[:, s, :, :].rearrange("p t f -> p (t f)")).then_inc(out_stored[s], 16)

            sp.dma_start(lb3[:, :], lin_b.to_broadcast([3, D])).then_inc(lin_b_loaded, 16)
            for h in range(2):
                sp.dma_start(xs[:, 0, h * BATCH // 2:(h + 1) * BATCH // 2, :].rearrange("p t f -> p (t f)"),
                             x_by_part[:, h * BL // 2:(h + 1) * BL // 2]).then_inc(first_loaded[h], 16)
            sp.dma_start(lw_sb[:, :], lin_w).then_inc(loaded, 16)
            sp.dma_start(dst_i[:, :], dst_cols).then_inc(loaded, 16)
            load(0, 1)
            load(0, 2)
            load(0, 3)
            sp.dma_start(src_i[:, :], src_cols).then_inc(e_loaded, 16)
            sp.dma_start(w1_sb[:, :], w1).then_inc(e_loaded, 16)
            sp.dma_start(w2_sb[:, :], w2).then_inc(e_loaded, 16)
            sp.dma_start(b1_sb[:, :], b1).then_inc(e_loaded, 16)
            sp.dma_start(b2_sb[:, :], b2).then_inc(e_loaded, 16)
            sp.wait_ge(ones_set, 1)
            sp.dma_start(out[DUMP:DUMP + QUAD * P, :].rearrange("(p t) f -> p (t f)", t=QUAD),
                         zero_rows[:, :]).then_inc(dump_stored, 16)

            def step(i, s, reused, more):
                if more:
                    free = (s + AHEAD) % XSLOTS
                    if reused:
                        sp.wait_ge(out_stored[free], 16 * (i + (s + AHEAD) // XSLOTS))
                    load(i + (s + AHEAD) // XSLOTS, free)
                store(i, s)

            for b in range(XSLOTS + 1):
                step(b // XSLOTS, b % XSLOTS, b + AHEAD >= XSLOTS, True)
            with sp.Fori(1, ROUNDS) as i:
                for b in range(1, XSLOTS + 1):
                    step(i + b // XSLOTS, b % XSLOTS, True, True)
            for b in range(ROUNDS * XSLOTS + 1, LAST - 1):
                step(b // XSLOTS, b % XSLOTS, True, b + AHEAD < NB)

            def load_attr(g, s):
                sp.dma_start(attr[:, s, :], attr_t[:, bass.ts(g, QUAD * P)]).then_inc(attr_loaded[s], 16)

            def edge_step(g, gm, more):
                if more:
                    sp.wait_ge(z_done, g + 1)
                    load_attr(g + RING, gm)
                sp.wait_ge(y_ready, g + 1)
                sp.dma_start(y_by_group[g], ysb[:, gm, :, :]).then_inc(y_stored[gm], 16)

            sp.wait_ge(out_stored[1], STORES[1])
            for g in range(RING):
                load_attr(g, g)
            store((LAST - 1) // XSLOTS, (LAST - 1) % XSLOTS)
            for q in range(QUADS):
                t = LAST * BATCH + q * QUAD
                sp.wait_ge(added[q], NB)
                sp.dma_start(out_by_part[:, t * D:(t + QUAD) * D],
                             xs[:, LAST % XSLOTS, q * QUAD:(q + 1) * QUAD, :].rearrange("p t f -> p (t f)")
                             ).then_inc(out_stored[LAST % XSLOTS], 16)
            with sp.Fori(0, (NG - 5) // RING) as i:
                for gm in range(RING):
                    edge_step(i * RING + gm, gm, True)
            for g in range(NG - 5, NG):
                edge_step(g, g % RING, g + RING < NG)
            for s in range(RING):
                sp.wait_ge(y_stored[s], 16 * ((NG - s + RING - 1) // RING))

            sp.wait_ge(slow_ready, 1)
            slow = sp.value_load(slow_i[0:1, 0:1], min_val=0, max_val=1)
            with sp.If(slow == 1):
                with sp.Fori(0, ET) as t:
                    sp.wait_ge(r_scattered, 16 * (t + 1))
                    sp.dma_start(ry[:, :], y_dram[bass.ts(t, P), :]).then_inc(r_y, 16)

        @block.gpsimd
        def _(pool):
            nc.gpsimd.memset(ident[:, :], 0.0).then_inc(const_made, 1)
            pool.wait_ge(const_made, 1)
            nc.gpsimd.affine_select(out=ident[:, :], in_=ident[:, :], compare_op=ALU.not_equal, fill=1.0,
                                    base=0, pattern=[[-1, P]], channel_multiplier=1).then_inc(const_made, 1)
            nc.gpsimd.iota(slot_row_i[:, :], [[1, P]], base=0, channel_multiplier=0).then_inc(const_made, 1)
            nc.gpsimd.iota(dump4_i[:, :], [[P, QUAD]], base=DUMP, channel_multiplier=1).then_inc(const_made, 1)
            nc.gpsimd.iota(edge_no_i[:, :], [[P, ET]], base=1, channel_multiplier=1).then_inc(const_made, 1)
            pool.wait_ge(ones_set, 2)
            nc.gpsimd.affine_select(out=before[:, WINDOW * P:], in_=before[:, WINDOW * P:],
                                    compare_op=ALU.is_gt, fill=0.0, base=0, pattern=[[-1, P]],
                                    channel_multiplier=1)
            nc.gpsimd.affine_select(out=below[:, :], in_=below[:, :], compare_op=ALU.is_gt, fill=0.0,
                                    base=0, pattern=[[1, P]], channel_multiplier=-1).then_inc(const_made, 1)
            pool.wait_ge(loaded, PREP)

            group_no = pool.alloc_register("group_no")
            landed_before = pool.alloc_register("landed_before")
            landed_now = pool.alloc_register("landed_now")
            round_no = pool.alloc_register("round_no")
            pool.reg_mov(group_no, 0)

            turned_no = pool.alloc_register("turned_no")
            rstd_no = pool.alloc_register("rstd_no")
            pool.reg_mov(rstd_no, 1)

            def norm(s, q, first):
                pool.wait_ge(const_made, 2)
                pool.wait_ge(rstd_ready, rstd_no)
                if not first:
                    pool.wait_ge(turned[q], turned_no)
                for k in range(QUAD - POOL_NORM[q], QUAD):
                    t = q * QUAD + k
                    last = nc.gpsimd.tensor_scalar(hn[:, q, k, :], xs[:, s, t, :], chain[:, s, 6, t:t + 1],
                                                   chain[:, s, 7, t:t + 1], ALU.mult, ALU.add)
                last.then_inc(hn_by_pool, 1)

            def gather(s, k):
                nc.gpsimd.indirect_dma_start(
                    gx[:, s % GSLOTS, k, :], None, x,
                    bass.IndirectOffsetOnAxis(ap=gidx[:, s, k:k + 1], axis=0)).then_inc(gathered[s % GSLOTS], 16)

            def node_step(b, s, first, more):
                s1 = (s + 1) % XSLOTS
                pool.reg_add(group_no, group_no, 1)
                pool.reg_add(turned_no, rstd_no, -1)
                nc.gpsimd.tensor_copy(gidx[:, s, :], dst_i[:, bass.ts(b, QUAD)]).then_inc(gidx_ready, 1)
                norm(s, 2, first)
                pool.wait_ge(loaded, PREP)
                pool.wait_ge(gidx_ready, group_no)
                gather(s, 0)
                norm(s, 3, first)
                gather(s, 1)
                if more:
                    pool.reg_add(turned_no, turned_no, 1)
                    pool.reg_add(rstd_no, rstd_no, 1)
                    norm(s1, 0, False)
                gather(s, 2)
                if more:
                    norm(s1, 1, False)
                gather(s, 3)

            norm(0, 0, True)
            norm(0, 1, True)
            node_step(0, 0, True, True)
            with pool.Fori(0, ROUNDS) as i:
                for b in range(1, XSLOTS + 1):
                    node_step(i * XSLOTS + b, b % XSLOTS, False, True)
            for b in range(ROUNDS * XSLOTS + 1, NB):
                node_step(b, b % XSLOTS, False, b < LAST)

            for s in range(XSLOTS):
                pool.wait_ge(out_stored[s], STORES[s])
            pool.wait_ge(dump_stored, 16)

            def scatter(s, first):
                pool.reg_add(group_no, group_no, 1)
                pool.reg_mov(landed_before, landed_now)
                pool.reg_add(landed_now, landed_now, 16)
                pool.wait_ge(dump_stored, 16)
                pool.wait_ge(y_ready, group_no)
                pool.wait_ge(sidx_ready, group_no)
                for k in range(QUAD):
                    if k == QUAD - 1 and not first:
                        pool.sem_inc(landed, 1)
                    pool.wait_ge(dump_stored, 16)
                    if k < QUAD - 1 and not first:
                        pool.wait_ge(scattered[k + 1], landed_before)
                    elif k == QUAD - 1:
                        pool.wait_ge(scattered[0], landed_now)
                    nc.gpsimd.indirect_dma_start(
                        out, bass.IndirectOffsetOnAxis(ap=sidx[:, s, k:k + 1], axis=0),
                        ysb[:, s, k, :], None, compute_op=ALU.add).then_inc(scattered[k], 16)

            pool.reg_mov(group_no, 0)
            pool.reg_mov(landed_now, 0)
            scatter(0, True)
            with pool.Fori(0, NG // LOOP) as i:
                for g in range(1, LOOP + 1):
                    scatter(g % RING, False)
            for g in range(NG // LOOP * LOOP + 1, NG):
                scatter(g % RING, False)

            pool.wait_ge(lidx_ready, 1)
            nc.gpsimd.indirect_dma_start(
                lsrc_i[:, :], None, src_rows,
                bass.IndirectOffsetOnAxis(ap=lidx[:, :], axis=0)).then_inc(lsrc_gathered, 16)
            for s in range(RING):
                pool.wait_ge(y_stored[s], 16 * ((NG - s + RING - 1) // RING))
            nc.gpsimd.indirect_dma_start(
                ry[:, :], None, y_dram,
                bass.IndirectOffsetOnAxis(ap=lidx[:, :], axis=0)).then_inc(ry_gathered, 16)
            for k in range(QUAD):
                pool.wait_ge(scattered[k], 16 * NG)

            def add_sums(n):
                pool.reg_add(round_no, round_no, 1)
                pool.wait_ge(dump_stored, 16)
                pool.wait_ge(r_ready, round_no)
                nc.gpsimd.indirect_dma_start(
                    out, bass.IndirectOffsetOnAxis(ap=ridx[:, :], axis=0),
                    rsum[:, :], None, compute_op=ALU.add).then_inc(r_scattered, 16)
                pool.wait_ge(r_scattered, 16 * (n + 1))

            pool.reg_mov(round_no, 0)
            add_sums(0)
            slow = pool.value_load(slow_i[0:1, 0:1], min_val=0, max_val=1)
            with pool.If(slow == 1):
                with pool.Fori(0, ET) as t:
                    add_sums(t + 1)

        @block.tensor
        def _(pe):
            pe.wait_ge(const_made, 2)
            pe.wait_ge(lin_b_ready, QUAD - 1)
            pe.wait_ge(loaded, PREP)

            def turn(b, q):
                pe.wait_ge(hn_by_act, b * QUADS + q + 1)
                pe.wait_ge(hn_by_pool, b * QUADS + q + 1)
                for k in range(QUAD):
                    last = nc.tensor.transpose(ps[:, q, k * P:(k + 1) * P], hn[:, q, k, :], ident[:, :])
                last.then_inc(turned[q], 1)

            def lin(b, q):
                pe.wait_ge(relu_done[q], b + 1)
                if not isinstance(b, int) or b:
                    pe.wait_ge(added[q], b)
                for k in range(QUAD):
                    nc.tensor.matmul(ps[:, QUADS + q, k * P:(k + 1) * P], hT[:, q, k * P:(k + 1) * P], lw_sb[:, :],
                                     start=(k == 0), stop=False, skip_group_check=True)
                nc.tensor.matmul(ps[:, QUADS + q, :], ones3[:, :], lb_sel[:, :, :].rearrange("p t f -> p (t f)"),
                                 start=False, stop=True, skip_group_check=True).then_inc(lin_done[q], 1)

            def z(g, gm):
                pe.wait_ge(attr_loaded[gm], 16 * (g // RING + 1) if isinstance(g, int) else 4 * (g - gm) + 16)
                if not isinstance(g, int) or g:
                    pe.wait_ge(z_relu, g)
                nc.tensor.matmul(ps[:, 0, :], w1_sb[:, :], attr[:, gm, :], start=True, stop=True).then_inc(z_done, 1)

            def node_step(b, more):
                turn(b, 2)
                lin(b, 0)
                turn(b, 3)
                lin(b, 1)
                if more:
                    turn(b + 1, 0)
                else:
                    pe.wait_ge(e_loaded, E_PREP)
                    z(0, 0)
                lin(b, 2)
                if more:
                    turn(b + 1, 1)
                lin(b, 3)

            turn(0, 0)
            turn(0, 1)
            node_step(0, True)
            with pe.Fori(0, ROUNDS) as i:
                for b in range(1, XSLOTS + 1):
                    node_step(i * XSLOTS + b, True)
            for b in range(ROUNDS * XSLOTS + 1, NB):
                node_step(b, b < LAST)

            def rows(g, gm):
                pe.wait_ge(srcg_ready, g + 1)
                if not isinstance(g, int) or g >= 2:
                    pe.wait_ge(clash_ready, g - 1)
                for k in range(WINDOW + QUAD):
                    last = nc.tensor.transpose(ps[:, 4 + 2 * (gm % 2) + k // QUAD, (k % QUAD) * P:(k % QUAD + 1) * P],
                                               srcg[:, gm, k:k + 1].to_broadcast([P, P]), ident[:, :])
                last.then_inc(rows_ready, 1)

            def e_lin(g, gm):
                pe.wait_ge(msg_ready, g + 1)
                if not isinstance(g, int) or g:
                    pe.wait_ge(y_ready, g)
                for k in range(QUAD):
                    last = nc.tensor.matmul(ps[:, 3, k * P:(k + 1) * P], msg[:, gm % 2, k * P:(k + 1) * P], lw_sb[:, :],
                                            start=True, stop=True, skip_group_check=True)
                last.then_inc(y_done, 1)

            def turn_edges(g, gm):
                pe.wait_ge(e_hn, g + 1)
                if not isinstance(g, int) or g:
                    pe.wait_ge(e_hT, g)
                for k in range(QUAD):
                    last = nc.tensor.transpose(ps[:, 2, k * P:(k + 1) * P], hne[:, gm % 2, k, :], ident[:, :])
                last.then_inc(e_turned, 1)

            def w(g, gm):
                pe.wait_ge(z_relu, g + 1)
                if not isinstance(g, int) or g:
                    pe.wait_ge(msg_ready, g)
                nc.tensor.matmul(ps[:, 1, :], w2_sb[:, :], z_sb[:, gm % 2, :], start=True, stop=True).then_inc(w_done, 1)

            def edge_step(g, gm, more):
                turn_edges(g, gm)
                if more:
                    z(g + 1, (gm + 1) % RING)
                w(g, gm)
                e_lin(g - 1, (gm + RING - 1) % RING)
                if more:
                    rows(g + 1, (gm + 1) % RING)

            pe.wait_ge(added[0], NB)
            pe.wait_ge(added[1], NB)
            rows(0, 0)
            turn_edges(0, 0)
            w(0, 0)
            z(1, 1)
            e_lin(0, 0)
            pe.wait_ge(added[2], NB)
            pe.wait_ge(added[3], NB)
            rows(1, 1)
            turn_edges(1, 1)
            z(2, 2)
            w(1, 1)
            rows(2, 2)
            with pe.Fori(0, (NG - 5) // RING) as i:
                for g in range(2, RING + 2):
                    edge_step(i * RING + g, g % RING, True)
            for g in range(NG - 3, NG):
                edge_step(g, g % RING, g + 1 < NG)
            e_lin(NG - 1, (NG - 1) % RING)

            pe.wait_ge(counts_ready, 1)
            nc.tensor.matmul(ps[:, 0, 0:1], below[:, :], cnt[:, 0:1], start=True, stop=True)
            nc.tensor.matmul(ps[:, 0, 2:4], ones[:, :], cnt[:, 0:2], start=True, stop=True).then_inc(base_ready, 1)
            pe.wait_ge(onehot_ready, 1)
            for k in range(TOP):
                last = nc.tensor.matmul(ps[:, 1, 0:1], onehot[:, k, :], top[:, k:k + 1],
                                        start=(k == 0), stop=(k == TOP - 1))
            last.then_inc(list_ready, 1)

            def sums(n, row_sem=None):
                pe.wait_ge(r_src, n + 1)
                nc.tensor.transpose(ps[:, 2, 0:P], rsrc[:, 0:1].to_broadcast([P, P]), ident[:, :]).then_inc(r_row, 1)
                pe.wait_ge(r_same, n + 1)
                if row_sem:
                    pe.wait_ge(row_sem, 16)
                nc.tensor.matmul(ps[:, 3, 0:D], same[:, :], ry[:, :], start=True, stop=True).then_inc(r_sum, 1)

            sums(0, ry_gathered)
            slow = pe.value_load(slow_i[0:1, 0:1], min_val=0, max_val=1)
            with pe.If(slow == 1):
                with pe.Fori(0, ET) as t:
                    pe.wait_ge(r_y, 16 * (t + 1))
                    sums(t + 1)

        @block.scalar
        def _(act):
            act.wait_ge(ones_set, 2)
            nc.scalar.activation(warm[:, :], ones[:, 0:1], ACT.Sqrt)

            def relu_quad(b, q):
                act.wait_ge(turned[q], b + 1)
                nc.scalar.activation(hT[:, q, :], ps[:, q, :], ACT.Relu).then_inc(relu_done[q], 1)

            def root(b, s):
                act.wait_ge(var_ready, b + 1)
                nc.scalar.activation(chain[:, s, 5, :], chain[:, s, 4, :], ACT.Sqrt, scale=1.0 / D).then_inc(sd_ready, 1)

            def norm(b, s, q, between=lambda: None):
                act.wait_ge(rstd_ready, b + 1)
                for k in range(QUAD - POOL_NORM[q]):
                    if k == QUAD - POOL_NORM[q] - 1:
                        between()
                    t = q * QUAD + k
                    last = nc.scalar.activation(hn[:, q, k, :], xs[:, s, t, :], ACT.Identity,
                                                bias=chain[:, s, 7, t:t + 1], scale=chain[:, s, 6, t:t + 1])
                last.then_inc(hn_by_act, 1)

            root(0, 0)
            norm(0, 0, 0)
            norm(0, 0, 1)

            def put(g, i, s):
                act.wait_ge(gathered[s % GSLOTS], 16 * QUAD * (i * (XSLOTS // GSLOTS) + s // GSLOTS + 1))
                nc.scalar.activation(xdst[:, bass.ts(g, QUAD), :].rearrange("p t f -> p (t f)"),
                                     gx[:, s % GSLOTS, :, :].rearrange("p t f -> p (t f)"), ACT.Copy).then_inc(xdst_by_act, 1)

            def node_step(i, s, last):
                b = i * XSLOTS + s
                s1 = (s + 1) % XSLOTS
                norm(b, s, 2, lambda: e_root(0, 0, 2 * QUAD) if last else root(b + 1, s1))
                relu_quad(b, 0)
                norm(b, s, 3)
                relu_quad(b, 1)
                if last:
                    relu_quad(b, 2)
                    relu_quad(b, 3)
                    return
                norm(b + 1, s1, 0)
                relu_quad(b, 2)
                norm(b + 1, s1, 1)
                if s % 2:
                    put(b - 1, i, s - 1)
                relu_quad(b, 3)

            def relu_z(g, s):
                act.wait_ge(z_done, g + 1)
                nc.scalar.activation(z_sb[:, s, :], ps[:, 0, :], ACT.Relu, bias=b1_sb[:, 0:1]).then_inc(z_relu, 1)

            def e_root(pair, h, n):
                act.wait_ge(e_var, pair + 1)
                nc.scalar.activation(chain[:, PAIR0 + h, 5, 0:n], chain[:, PAIR0 + h, 4, 0:n], ACT.Sqrt,
                                     scale=1.0 / D).then_inc(e_sd, 1)

            def e_norm(g, gm):
                act.wait_ge(e_rstd, g // 2 + 1 if isinstance(g, int) else half(g, gm) + 1)
                for k in range(QUAD):
                    c = (gm % 2) * QUAD + k
                    last = nc.scalar.activation(hne[:, gm % 2, k, :],
                                                xdst[:, bass.ds(g * QUAD + k, 1), :].rearrange("p t f -> p (t f)"),
                                                ACT.Identity, bias=chain[:, PAIR0 + gm // 2, 7, c:c + 1],
                                                scale=chain[:, PAIR0 + gm // 2, 6, c:c + 1])
                last.then_inc(e_hn, 1)

            node_step(0, 0, False)
            with act.Fori(0, ROUNDS) as i:
                for b in range(1, XSLOTS + 1):
                    node_step(i + b // XSLOTS, b % XSLOTS, False)
            for b in range(ROUNDS * XSLOTS + 1, NB):
                node_step(b // XSLOTS, b % XSLOTS, b == LAST)

            act.wait_ge(e_loaded, E_PREP)
            act.wait_ge(out_stored[2], STORES[2])
            e_norm(0, 0)
            relu_z(0, 0)

            def y_rows(g, gm, reused):
                act.wait_ge(y_done, g + 1)
                if reused:
                    act.wait_ge(landed, g - 3)
                    act.wait_ge(y_stored[gm], 4 * (g - gm))
                nc.scalar.activation(ysb[:, gm, :, :].rearrange("p t f -> p (t f)"), ps[:, 3, :],
                                     ACT.Copy).then_inc(y_ready, 1)

            def edge_step(g, gm, pair, more, root_n, reused):
                act.wait_ge(e_turned, g + 1)
                nc.scalar.activation(hTe[:, gm % 2, :], ps[:, 2, :], ACT.Relu).then_inc(e_hT, 1)
                if more:
                    relu_z(g + 1, (gm + 1) % 2)
                    e_norm(g + 1, (gm + 1) % RING)
                if isinstance(g, int) and g == 0:
                    y_rows(0, 0, False)
                elif isinstance(g, int) and g == 1:
                    put(LAST, LAST // XSLOTS, LAST % XSLOTS)
                else:
                    y_rows(g - 1, (gm + RING - 1) % RING, reused)
                if root_n:
                    e_root(pair + 1, ((gm + 2) % RING) // 2, root_n)

            def peeled(g):
                root_n = 0 if g % 2 or g + 2 >= NG else QUAD * min(2, NG - g - 2)
                edge_step(g, g % RING, g // 2, g + 1 < NG, root_n, g >= 5)

            for g in range(6):
                peeled(g)
            with act.Fori(1, (NG - 5) // RING) as i:
                for g in range(2, RING + 2):
                    edge_step(i * RING + g, g % RING, i * 2 + g // 2, True, 0 if g % 2 else 2 * QUAD, True)
            for g in range(NG - 3, NG):
                peeled(g)
            y_rows(NG - 1, (NG - 1) % RING, True)

        @block.vector
        def _(dve):
            nc.vector.memset(zero_rows[:, :], 0.0).then_inc(ones_set, 1)
            nc.vector.memset(ones[:, :], 1.0)
            nc.vector.memset(below[:, :], 1.0)
            nc.vector.memset(before[:, :], 1.0).then_inc(ones_set, 1)
            nc.vector.memset(ones3[:, :], 1.0)
            nc.vector.memset(src_f[:, 0:WINDOW], -1.0)
            done = [0]

            def then(ins):
                done[0] += 1
                ins.then_inc(prep, 1)

            def on():
                dve.wait_ge(prep, done[0])
                return nc.vector

            def prep_steps():
                first, second, third = lb_part[:, 0, :], lb_part[:, 1, :], lb_part[:, 2, :]
                sel = lb_sel[:, 0, :]

                def start():
                    dve.wait_ge(lin_b_loaded, 16)
                    dve.wait_ge(const_made, 2)
                    then(nc.vector.tensor_copy(first, lb3[:, :]))

                return [
                    start,
                    lambda: then(on().tensor_tensor(lb_res[:, :], lb3[:, :], first, ALU.subtract)),
                    lambda: then(on().tensor_copy(second, lb_res[:, :])),
                    lambda: then(on().tensor_tensor(lb_res[:, :], lb_res[:, :], second, ALU.subtract)),
                    lambda: then(on().tensor_copy(third, lb_res[:, :])),
                    lambda: then(on().tensor_scalar(sel, first, ident[0:3, 0:1], None, ALU.mult)),
                    lambda: then(on().scalar_tensor_tensor(out=sel, in0=second, scalar=ident[0:3, 1:2], in1=sel,
                                                        op0=ALU.mult, op1=ALU.add)),
                    lambda: then(on().scalar_tensor_tensor(out=sel, in0=third, scalar=ident[0:3, 2:3], in1=sel,
                                                        op0=ALU.mult, op1=ALU.add)),
                ]

            def chain_steps(n, h, b, done, var_sem, sd_sem, rstd_sem):
                STEPS = 8

                def after(k):
                    dve.wait_ge(done, b * STEPS + k)
                st = stat[:, h, 0:n, :]
                c = lambda r: chain[:, h, r, 0:n]

                def halves():
                    nc.vector.tensor_tensor(c(1), st[:, :, 1], st[:, :, 4], ALU.subtract).then_inc(done, 1)
                    nc.vector.tensor_tensor(c(2), st[:, :, 2], st[:, :, 5], ALU.add).then_inc(done, 1)
                    nc.vector.tensor_tensor(c(0), st[:, :, 1], st[:, :, 4], ALU.add).then_inc(done, 1)

                def between():
                    after(1)
                    nc.vector.scalar_tensor_tensor(out=c(3), in0=c(1), scalar=float(D // 4), in1=c(1),
                                                   op0=ALU.mult, op1=ALU.mult).then_inc(done, 1)

                def total():
                    after(4)
                    nc.vector.scalar_tensor_tensor(out=c(4), in0=c(2), scalar=float(D * EPS), in1=c(3),
                                                   op0=ALU.add, op1=ALU.add).then_inc(var_sem, 1)

                def inverse():
                    dve.wait_ge(sd_sem, b + 1)
                    nc.vector.reciprocal(c(1), c(5)).then_inc(done, 1)

                def newton1():
                    after(5)
                    nc.vector.tensor_tensor(c(2), c(1), c(1), ALU.mult).then_inc(done, 1)

                def newton2():
                    after(6)
                    nc.vector.scalar_tensor_tensor(out=c(3), in0=c(2), scalar=-0.5 / D, in1=c(4),
                                                   op0=ALU.mult, op1=ALU.mult).then_inc(done, 1)

                def newton3():
                    after(7)
                    nc.vector.scalar_tensor_tensor(out=c(6), in0=c(3), scalar=1.5, in1=c(1),
                                                   op0=ALU.add, op1=ALU.mult).then_inc(done, 1)

                def shift():
                    after(8)
                    nc.vector.scalar_tensor_tensor(out=c(7), in0=c(0), scalar=-0.5, in1=c(6),
                                                   op0=ALU.mult, op1=ALU.mult).then_inc(rstd_sem, 1)

                return halves, between, total, inverse, newton1, newton2, newton3, shift

            def add_quad(b, s, q):
                dve.wait_ge(lin_done[q], b + 1)
                x_quad = xs[:, s, q * QUAD:(q + 1) * QUAD, :].rearrange("p t f -> p (t f)")
                nc.vector.tensor_tensor(x_quad, ps[:, QUADS + q, :], x_quad, ALU.add).then_inc(added[q], 1)

            def bn(s, *tiles):
                for t in tiles:
                    ins = nc.vector.bn_stats(stat[:, s, t, :], xs[:, s, t, :])
                    if t == BATCH - 1:
                        ins.then_inc(stats_ready, 1)

            def put(g, i, s):
                dve.wait_ge(gathered[s % GSLOTS], 16 * QUAD * (i * (XSLOTS // GSLOTS) + s // GSLOTS + 1))
                nc.vector.tensor_copy(xdst[:, bass.ts(g, QUAD), :].rearrange("p t f -> p (t f)"),
                                      gx[:, s % GSLOTS, :, :].rearrange("p t f -> p (t f)")).then_inc(xdst_by_dve, 1)

            def node_step(i, s, first, bn_more, instead=None, first_edge_steps=None):
                b = i * XSLOTS + s
                s1, s2 = (s + 1) % XSLOTS, (s + 2) % XSLOTS

                def stats(*tiles):
                    if bn_more:
                        bn(s2, *tiles)
                    else:
                        for t in tiles:
                            instead(t)

                steps = chain_steps(BATCH, s1, b + 1, chain_step, var_ready, sd_ready, rstd_ready)
                if bn_more:
                    dve.wait_ge(x_loaded[s2], 16 * (i + (s + 2) // XSLOTS + (1 if s2 else 0)))
                    next_steps = chain_steps(BATCH, s2, b + 2, chain_step, var_ready, sd_ready, rstd_ready)
                else:
                    next_steps = first_edge_steps
                stats(0, 1)
                steps[3]()
                stats(2)
                steps[4]()
                stats(3)
                steps[5]()
                if not first:
                    add_quad(b - 1, (s + XSLOTS - 1) % XSLOTS, 3)
                steps[6]()
                stats(4)
                steps[7]()
                stats(5, 6, 7)
                add_quad(b, s, 0)
                stats(8, 9, 10, 11, 12)
                add_quad(b, s, 1)
                stats(13, 14, 15)
                if not first and s % 2 == 0:
                    put(b - 1, i if s else i - 1, (s + XSLOTS - 1) % XSLOTS)
                if bn_more:
                    dve.wait_ge(stats_ready, b + 3)
                else:
                    dve.wait_ge(e_stats, 2)
                next_steps[0]()
                next_steps[1]()
                add_quad(b, s, 2)
                next_steps[2]()

            steps = prep_steps()
            early = len(steps) // 2
            for step in steps[:early]:
                step()
            for t in range(BATCH):
                if t % (BATCH // 2) == 0:
                    dve.wait_ge(first_loaded[t // (BATCH // 2)], 16)
                bn(0, t)
                if t < len(steps) - early:
                    steps[early + t]()
            for k in range(1, QUAD):
                on().tensor_copy(lb_sel[:, k, :], lb_sel[:, 0, :]).then_inc(lin_b_ready, 1)
            dve.wait_ge(stats_ready, 1)
            for step in chain_steps(BATCH, 0, 0, chain_step, var_ready, sd_ready, rstd_ready):
                step()
            dve.wait_ge(x_loaded[1], 16)
            bn(1, *range(BATCH))
            dve.wait_ge(stats_ready, 2)
            for step in chain_steps(BATCH, 1, 1, chain_step, var_ready, sd_ready, rstd_ready)[:3]:
                step()
            node_step(0, 0, True, True)
            with dve.Fori(0, ROUNDS) as i:
                for b in range(1, XSLOTS + 1):
                    node_step(i + b // XSLOTS, b % XSLOTS, False, True)
            def e_bn(g, gm, k):
                ins = nc.vector.bn_stats(stat[:, PAIR0 + gm // 2, (gm % 2) * QUAD + k, :],
                                         xdst[:, bass.ds(g * QUAD + k, 1), :].rearrange("p t f -> p (t f)"))
                if k == QUAD - 1:
                    ins.then_inc(e_stats, 1)

            def e_bn_group(g):
                for k in range(QUAD):
                    e_bn(g, g, k)

            def sources(g, gm):
                if not isinstance(g, int) or g >= RING:
                    dve.wait_ge(sidx_ready, g - 3)
                nc.vector.tensor_copy(srcg[:, gm, :], src_f[:, bass.ds(g * QUAD, WINDOW + QUAD)]).then_inc(srcg_ready, 1)

            def clashes(g, gm, k):
                both = ps[:, 4 + 2 * (gm % 2):6 + 2 * (gm % 2), :].rearrange("p b c -> p (b c)")
                last = nc.vector.scalar_tensor_tensor(
                    out=eqs[:, k, :], in0=both[:, k * P:(k + WINDOW + 1) * P], scalar=srcg[:, gm, WINDOW + k:WINDOW + k + 1],
                    in1=before[:, :], op0=ALU.is_equal, op1=ALU.mult, accum_out=clash[:, gm, k:k + 1])
                if k == QUAD - 1:
                    last.then_inc(clash_ready, 1)

            def targets(g, gm, reused):
                group_off = off[:, bass.ds(g * QUAD, QUAD)]

                def put_off():
                    dve.wait_ge(clash_ready, g + 1)
                    nc.vector.scalar_tensor_tensor(out=group_off, in0=clash[:, gm, :], scalar=1.0, in1=group_off,
                                                   op0=ALU.min, op1=ALU.mult).then_inc(off_ready, 1)

                def target():
                    if reused:
                        dve.wait_ge(landed, g - 3)
                    dve.wait_ge(off_ready, g + 1)
                    nc.vector.tensor_tensor(sidx[:, gm, :], group_off, srcg[:, gm, WINDOW:], ALU.add).then_inc(sidx_ready, 1)

                return put_off, target

            def message(g, s):
                dve.wait_ge(w_done, g + 1)
                dve.wait_ge(e_hT, g + 1)
                if not isinstance(g, int) or g >= 2:
                    dve.wait_ge(y_done, g - 1)
                nc.vector.scalar_tensor_tensor(out=msg[:, s, :], in0=ps[:, 1, :], scalar=b2_sb[:, 0:1], in1=hTe[:, s, :],
                                               op0=ALU.add, op1=ALU.mult).then_inc(msg_ready, 1)

            def edge_step(g, gm, pair, chain_n, bn_more, src_more, reused):
                even = gm % 2 == 0
                slot = ((gm - gm % 2 + 2) % RING) // 2
                none = [lambda: None] * 8
                steps = chain_steps(chain_n, PAIR0 + slot, pair + 1, e_chain, e_var, e_sd, e_rstd) if chain_n else none
                start, finish = (steps, none) if even else (none, steps)
                put_off, target = targets(g, gm, reused)

                def stats(k):
                    if bn_more:
                        e_bn(g + 4, gm, k)

                if isinstance(g, int) and g == 2:
                    dve.wait_ge(xdst_by_act, (NG + 1) // 2)
                    dve.wait_ge(xdst_by_dve, NG // 2)
                if even and chain_n:
                    dve.wait_ge(e_stats, g + (4 if chain_n == 2 * QUAD else 3))
                first = isinstance(g, int) and g == 0
                finish[4]()
                if first:
                    message(0, 0)
                dve.wait_ge(rows_ready, g + 1)
                start[0]()
                clashes(g, gm, 0)
                finish[5]()
                stats(0)
                finish[6]()
                if not even:
                    stats(1)
                finish[7]()
                start[1]()
                clashes(g, gm, 1)
                if even:
                    stats(1)
                start[2]()
                clashes(g, gm, 2)
                stats(2)
                clashes(g, gm, 3)
                stats(3)
                if not first:
                    message(g, gm % 2)
                start[3]()
                put_off()
                if src_more:
                    sources(g + 2, (gm + 2) % RING)
                target()
                if isinstance(g, int) and g == 0:
                    put(LAST - 1, (LAST - 1) // XSLOTS, (LAST - 1) % XSLOTS)

            def peeled(g):
                left = NG - (g - g % 2) - 2
                edge_step(g, g % RING, g // 2, QUAD * min(2, left) if left > 0 else 0, g + 4 < NG, g + 2 < NG,
                          g >= RING)

            for b in range(ROUNDS * XSLOTS + 1, LAST - 1):
                node_step(b // XSLOTS, b % XSLOTS, False, True)

            def first_edges(t):
                if t < 2 * QUAD:
                    if t == 0:
                        dve.wait_ge(xdst_by_act, 3)
                        dve.wait_ge(xdst_by_dve, 3)
                    e_bn(t // QUAD, t // QUAD, t % QUAD)
                elif t == 2 * QUAD:
                    dve.wait_ge(e_loaded, E_PREP)
                    dve.wait_ge(const_made, N_CONST)
                    nc.vector.tensor_copy(src_f[:, WINDOW:], src_i[:, :]).then_inc(src_ready, 1)
                    nc.vector.tensor_copy(slot_row[:, :], slot_row_i[:, :])
                    nc.vector.tensor_copy(dump4[:, :], dump4_i[:, :]).then_inc(src_ready, 1)
                    nc.vector.tensor_copy(edge_no[:, :], edge_no_i[:, :]).then_inc(src_ready, 1)

            steps = chain_steps(2 * QUAD, PAIR0, 0, e_chain, e_var, e_sd, e_rstd)
            node_step((LAST - 1) // XSLOTS, (LAST - 1) % XSLOTS, False, False, first_edges, steps)
            dve.wait_ge(src_ready, 3)
            nc.vector.tensor_tensor(off[:, :].rearrange("p (g t) -> p g t", t=QUAD),
                                    dump4[:, None, :].to_broadcast([P, NG, QUAD]),
                                    src_f[:, WINDOW:].rearrange("p (g t) -> p g t", t=QUAD),
                                    ALU.subtract).then_inc(src_ready, 1)
            sources(0, 0)
            sources(1, 1)
            add_quad(LAST - 1, (LAST - 1) % XSLOTS, 3)
            e_bn_group(2)
            steps[3]()
            add_quad(LAST, LAST % XSLOTS, 0)
            for step in steps[4:]:
                step()
            e_bn_group(3)
            for q in range(1, QUADS):
                add_quad(LAST, LAST % XSLOTS, q)
            dve.wait_ge(src_ready, 4)
            dve.wait_ge(out_stored[3], STORES[3])
            for g in range(RING):
                peeled(g)
            with dve.Fori(0, (NG - 9) // LOOP) as i:
                for g in range(RING, RING + LOOP):
                    edge_step(i * LOOP + g, g % RING, i * RING + g // 2, 2 * QUAD, True, True, True)
            for g in range(RING + (NG - 9) // LOOP * LOOP, NG):
                peeled(g)

            packed = [0]

            def link(ins):
                packed[0] += 1
                ins.then_inc(pack_step, 1)
                dve.wait_ge(pack_step, packed[0])

            dve.wait_ge(off_ready, NG)
            link(nc.vector.scalar_tensor_tensor(out=keys[:, :], in0=off[:, :], scalar=0.0, in1=edge_no[:, :],
                                                op0=ALU.is_gt, op1=ALU.mult))
            link(nc.vector.max(top[:, :], keys[:, :]))
            link(nc.vector.tensor_scalar(pos[:, 0, :], top[:, :], 0.0, None, ALU.is_gt))
            link(nc.vector.tensor_reduce(cnt[:, 0:1], pos[:, 0, :], AX_X, ALU.add))
            link(nc.vector.tensor_scalar(flags[:, :], keys[:, :], 0.0, None, ALU.is_gt))
            nc.vector.tensor_reduce(cnt[:, 1:2], flags[:, :], AX_X, ALU.add).then_inc(counts_ready, 1)
            dve.wait_ge(base_ready, 1)
            link(nc.vector.tensor_copy(cnt[:, 2:3], ps[:, 0, 0:1]))
            link(nc.vector.tensor_scalar(pos[:, 1, :], slot_row[:, 0:TOP], cnt[:, 2:3], 1.0, ALU.add, ALU.add))
            link(nc.vector.tensor_tensor(pos[:, 2, :], pos[:, 1, :], pos[:, 0, :], ALU.mult))
            link(nc.vector.tensor_scalar(pos[:, 3, :], pos[:, 2, :], 1.0, None, ALU.subtract))
            for k in range(TOP):
                last = nc.vector.tensor_scalar(onehot[:, k, :], slot_row[:, :], pos[:, 3, k:k + 1], None, ALU.is_equal)
            last.then_inc(onehot_ready, 1)
            link(nc.vector.tensor_copy(cnt[:, 3:5], ps[:, 0, 2:4]))
            link(nc.vector.tensor_tensor(cnt[:, 5:6], cnt[:, 4:5], cnt[:, 3:4], ALU.is_gt))
            link(nc.vector.tensor_scalar(cnt[:, 6:7], cnt[:, 4:5], float(P), None, ALU.is_gt))
            link(nc.vector.tensor_tensor(cnt[:, 5:6], cnt[:, 5:6], cnt[:, 6:7], ALU.max))
            link(nc.vector.tensor_copy(slow_i[:, :], cnt[:, 5:6]))
            link(nc.vector.tensor_scalar(cnt[:, 6:7], cnt[:, 5:6], -1.0, 1.0, ALU.mult, ALU.add))
            dve.wait_ge(list_ready, 1)
            link(nc.vector.tensor_copy(lkey[:, 0:1], ps[:, 1, 0:1]))
            link(nc.vector.tensor_scalar(lkey[:, 1:2], lkey[:, 0:1], 1.0, None, ALU.min))
            link(nc.vector.tensor_tensor(lkey[:, 2:3], lkey[:, 0:1], lkey[:, 1:2], ALU.subtract))
            nc.vector.tensor_copy(lidx[:, :], lkey[:, 2:3]).then_inc(lidx_ready, 1)
            link(nc.vector.tensor_tensor(lkey[:, 1:2], lkey[:, 1:2], cnt[:, 6:7], ALU.mult))
            dve.wait_ge(lsrc_gathered, 16)
            dump = dump4[:, QUAD - 1:QUAD]

            def pick(source, taken, n, wait):
                wait(nc.vector.tensor_tensor(rsrc[:, 1:2], source, dump, ALU.subtract))
                wait(nc.vector.tensor_tensor(rsrc[:, 2:3], rsrc[:, 1:2], taken, ALU.mult))
                nc.vector.tensor_tensor(rsrc[:, 0:1], rsrc[:, 2:3], dump, ALU.add).then_inc(r_src, 1)

            def sums(n, wait):
                dve.wait_ge(r_src, n + 1)
                dve.wait_ge(r_row, n + 1)
                nc.vector.tensor_scalar(same[:, :], ps[:, 2, 0:P], rsrc[:, 0:1], None, ALU.is_equal).then_inc(r_same, 1)
                wait(nc.vector.scalar_tensor_tensor(out=eqs[:, 0, 0:P], in0=ps[:, 2, 0:P], scalar=rsrc[:, 0:1],
                                                    in1=before[:, WINDOW * P:], op0=ALU.is_equal, op1=ALU.mult,
                                                    accum_out=lkey[:, 3:4]))
                wait(nc.vector.tensor_tensor(rsrc[:, 1:2], dump, rsrc[:, 0:1], ALU.subtract))
                wait(nc.vector.scalar_tensor_tensor(out=rsrc[:, 2:3], in0=lkey[:, 3:4], scalar=1.0, in1=rsrc[:, 1:2],
                                                    op0=ALU.min, op1=ALU.mult))
                wait(nc.vector.tensor_tensor(ridx[:, :], rsrc[:, 2:3], rsrc[:, 0:1], ALU.add))
                dve.wait_ge(r_sum, n + 1)
                nc.vector.tensor_copy(rsum[:, :], ps[:, 3, 0:D]).then_inc(r_ready, 1)

            link(nc.vector.tensor_copy(rsrc[:, 3:4], lsrc_i[:, :]))
            pick(rsrc[:, 3:4], lkey[:, 1:2], 0, link)
            sums(0, link)
            dve.sem_inc(slow_ready, 1)

            slow = dve.value_load(slow_i[0:1, 0:1], min_val=0, max_val=1)
            with dve.If(slow == 1):
                with dve.Fori(0, ET) as t:
                    n = t + 1
                    k = [0]

                    def turn(ins):
                        k[0] += 1
                        ins.then_inc(r_step, 1)
                        dve.wait_ge(r_step, t * 8 + k[0])

                    dve.wait_ge(r_scattered, 16 * n)
                    turn(nc.vector.tensor_scalar(lkey[:, 1:2], keys[:, bass.ds(t, 1)], 1.0, None, ALU.min))
                    turn(nc.vector.tensor_copy(rsrc[:, 3:4], src_f[:, bass.ds(t + WINDOW, 1)]))
                    pick(rsrc[:, 3:4], lkey[:, 1:2], n, turn)
                    sums(n, turn)


_INS = ["x", "src_cols", "src_rows", "dst_cols", "attr_t", "w1", "b1", "w2", "b2", "lin_w", "lin_b"]


def kernel(x, src, dst, edge_attr_50, edge_weight, L0_gnn_mlp_w1, L0_gnn_mlp_b1, L0_gnn_mlp_w2, L0_gnn_mlp_b2,
           L0_gnn_lin_w, L0_gnn_lin_b):
    import numpy as np
    import concourse.bacc as bacc
    from concourse.bass_utils import run_bass_kernel_spmd

    nodes, feats = x.shape
    edges = src.shape[0]
    nt, et = node_tiles(nodes), edge_tiles(edges)

    def padded(a, rows, fill):
        full = np.empty((rows,) + a.shape[1:], a.dtype)
        full[:a.shape[0]] = a
        full[a.shape[0]:] = fill
        return full

    pads = np.arange(edges, et * P)
    dump_rows = (nt * P + (pads // P % QUAD) * P + pads % P).astype(np.int32)
    src_p = padded(np.asarray(src), et * P, dump_rows)
    dst_p = padded(np.asarray(dst), et * P, 0)
    attr_p = padded(np.asarray(edge_attr_50), et * P, 0)
    arrays = {
        "x": padded(np.asarray(x), nt * P, 0),
        "src_cols": np.ascontiguousarray(src_p.reshape(et, P).T),
        "src_rows": src_p.reshape(et * P, 1),
        "dst_cols": np.ascontiguousarray(dst_p.reshape(et, P).T),
        "attr_t": np.ascontiguousarray(attr_p.T),
        "w1": np.asarray(L0_gnn_mlp_w1),
        "b1": np.asarray(L0_gnn_mlp_b1).reshape(-1, 1),
        "w2": np.asarray(L0_gnn_mlp_w2),
        "b2": np.asarray(L0_gnn_mlp_b2).reshape(-1, 1),
        "lin_w": np.asarray(L0_gnn_lin_w),
        "lin_b": np.asarray(L0_gnn_lin_b).reshape(1, -1),
    }
    nc = bacc.Bacc("TRN2", target_bir_lowering=False, num_devices=1)
    args = [nc.dram_tensor(n + "_dram", arrays[n].shape, mybir.dt.from_np(arrays[n].dtype), kind="ExternalInput").ap()
            for n in _INS]
    y_dram = nc.dram_tensor("y_dram", (et * P, feats), F32).ap()
    out = nc.dram_tensor("out_dram", (nt * P + QUAD * P, feats), F32, kind="ExternalOutput").ap()
    build(nc, *args, y_dram, out)
    r = run_bass_kernel_spmd(nc, [{n + "_dram": arrays[n] for n in _INS}], core_ids=[0])
    return r.results[0]["out_dram"][:nodes]
```
